# Optimizing a Trainium2 kernel written in Bass

```python
import numpy as np
import jax
import jax.numpy as jnp

def _softmax(x, axis=-1):
    return jax.nn.softmax(x, axis=axis)

def _gelu(x):
    return jax.nn.gelu(x, approximate=True)

def _silu(x):
    return jax.nn.silu(x)

def _sigmoid(x):
    return jax.nn.sigmoid(x)

def _layernorm(x, axis=-1, eps=1e-05):
    m = jnp.mean(x, axis=axis, keepdims=True)
    v = jnp.var(x, axis=axis, keepdims=True)
    return (x - m) / jnp.sqrt(v + eps)

def _scatter_add(tgt, idx, src, axis=0):
    return tgt.at[idx].add(src)

def _segment_sum(src, seg, n):
    return jax.ops.segment_sum(src, seg, n)
kernel_name = 'mk_audio_tower_d1_tok_audfeat256_r4_dc9c22'

def setup_inputs(seed: int=0):
    np.random.seed(seed)
    _w = jnp.asarray

    def _rec_inputs():
        import jax
        import jax.numpy as jnp
        _rk = jax.random.key(seed)
        x = -0.000392918 + 0.999932 * jax.random.normal(jax.random.fold_in(_rk, 1), (8, 750, 64), jnp.float32)
        return x
    x = _rec_inputs()

    def _L0_tok_setup():
        import jax, jax.numpy as jnp
        import numpy as np
        from jax import lax
        B, S, CIN, COUT, K = (32, 512, 64, 64, 16)
        key = jax.random.key(seed)
        k1, k2, k3, k4 = jax.random.split(key, 4)
        x = jax.random.normal(k1, (B, S, CIN), dtype=jnp.float32)
        w_real = jax.random.normal(k2, (COUT, CIN, K), dtype=jnp.float32) * 0.1
        w_imag = jax.random.normal(k3, (COUT, CIN, K), dtype=jnp.float32) * 0.1
        phases = jax.random.normal(k4, (K,), dtype=jnp.float32) * 0.1
        return {'x': x, 'w_real': w_real, 'w_imag': w_imag, 'phases': phases}
    _L0_tok_all = _L0_tok_setup()
    _L0_tok_in = {k: v for k, v in _L0_tok_all.items() if k in ('w_real', 'w_imag', 'phases')}
    del _L0_tok_all

    def _L0_attn_setup():
        import jax, jax.numpy as jnp
        import numpy as np
        key = jax.random.key(seed)
        k1, k2, k3 = jax.random.split(key, 3)
        d = 64
        x = jax.random.normal(k1, (8, 512, d), dtype=jnp.float32)
        Wq = jax.random.normal(k2, (d, d), dtype=jnp.float32) * d ** (-0.5)
        Wk = jax.random.normal(k3, (d, d), dtype=jnp.float32) * d ** (-0.5)
        return {'x': x, 'Wq': Wq, 'Wk': Wk}
    _L0_attn_all = _L0_attn_setup()
    _L0_attn_in = {k: v for k, v in _L0_attn_all.items() if k in ('Wq', 'Wk')}
    del _L0_attn_all

    def _L0_ffn_setup():
        import jax, jax.numpy as jnp
        import numpy as np
        B, S, H, F, E, K = (8, 1024, 64, 128, 16, 2)
        EPS = 1e-05
        key = jax.random.key(seed)
        ks = jax.random.split(key, 9)
        sc = 0.02
        return {'x': jax.random.normal(ks[0], (B, S, H), dtype=jnp.float32), 'gate_w': jax.random.normal(ks[1], (H, E), dtype=jnp.float32) * sc, 'gate_b': jnp.zeros((E,), dtype=jnp.float32), 'w1': jax.random.normal(ks[2], (E, H, F), dtype=jnp.float32) * sc, 'b1': jnp.zeros((E, F), dtype=jnp.float32), 'w2': jax.random.normal(ks[3], (E, F, H), dtype=jnp.float32) * sc, 'b2': jnp.zeros((E, H), dtype=jnp.float32), 'gamma': jnp.ones((H,), dtype=jnp.float32), 'beta': jnp.zeros((H,), dtype=jnp.float32)}
    _L0_ffn_all = _L0_ffn_setup()
    _L0_ffn_in = {k: v for k, v in _L0_ffn_all.items() if k in ('gate_w', 'gate_b', 'w1', 'b1', 'w2', 'b2', 'gamma', 'beta')}
    del _L0_ffn_all
    return {'x': x, 'L0_tok_w_real': _L0_tok_in['w_real'], 'L0_tok_w_imag': _L0_tok_in['w_imag'], 'L0_tok_phases': _L0_tok_in['phases'], 'L0_attn_Wq': _L0_attn_in['Wq'], 'L0_attn_Wk': _L0_attn_in['Wk'], 'L0_ffn_gate_w': _L0_ffn_in['gate_w'], 'L0_ffn_gate_b': _L0_ffn_in['gate_b'], 'L0_ffn_w1': _L0_ffn_in['w1'], 'L0_ffn_b1': _L0_ffn_in['b1'], 'L0_ffn_w2': _L0_ffn_in['w2'], 'L0_ffn_b2': _L0_ffn_in['b2'], 'L0_ffn_gamma': _L0_ffn_in['gamma'], 'L0_ffn_beta': _L0_ffn_in['beta']}

def reference(x, L0_tok_w_real, L0_tok_w_imag, L0_tok_phases, L0_attn_Wq, L0_attn_Wk, L0_ffn_gate_w, L0_ffn_gate_b, L0_ffn_w1, L0_ffn_b1, L0_ffn_w2, L0_ffn_b2, L0_ffn_gamma, L0_ffn_beta):
    import jax
    import jax.numpy as jnp

    def _L0_tok_ref(x, w_real, w_imag, phases):
        import jax, jax.numpy as jnp
        import numpy as np
        from jax import lax
        B, S, CIN, COUT, K = (32, 512, 64, 64, 16)
        w_eff = jnp.cos(phases)[None, None, :] * w_real - jnp.sin(phases)[None, None, :] * w_imag
        y = lax.conv_general_dilated(jnp.transpose(x, (0, 2, 1)), w_eff, window_strides=(1,), padding='VALID', dimension_numbers=('NCH', 'OIH', 'NCH'))
        return jnp.transpose(y, (0, 2, 1))

    def _L0_attn_ref(x, Wq, Wk):
        import jax, jax.numpy as jnp
        import numpy as np
        d = x.shape[-1]
        scale = d ** (-0.5)
        q = jnp.einsum('bnd,ed->bne', x, Wq)
        k = jnp.einsum('bnd,ed->bne', x, Wk)
        sim = jnp.einsum('bid,bjd->bij', q, k) * scale
        attn = jax.nn.softmax(sim, axis=-1)
        out = jnp.einsum('bij,bjd->bid', attn, x)
        return out

    def _L0_ffn_ref(x, gate_w, gate_b, w1, b1, w2, b2, gamma, beta):
        import jax, jax.numpy as jnp
        import numpy as np
        B, S, H, F, E, K = (8, 1024, 64, 128, 16, 2)
        EPS = 1e-05
        gate_logits = x @ gate_w + gate_b
        topk_vals, topk_idx = jax.lax.top_k(gate_logits, K)
        topk_w = jax.nn.softmax(topk_vals, axis=-1)
        h = jax.nn.relu(jnp.einsum('bsh,ehf->bsef', x, w1) + b1)
        expert_out = jnp.einsum('bsef,efh->bseh', h, w2) + b2
        sel = jnp.take_along_axis(expert_out, topk_idx[:, :, :, None], axis=2)
        moe = jnp.sum(topk_w[..., None] * sel, axis=2)
        y = x + moe
        mu = jnp.mean(y, axis=-1, keepdims=True)
        var = jnp.var(y, axis=-1, keepdims=True)
        return (y - mu) / jnp.sqrt(var + EPS) * gamma + beta
    h = _L0_tok_ref(x, L0_tok_w_real, L0_tok_w_imag, L0_tok_phases)
    h = h + _L0_attn_ref(_layernorm(h, axis=-1), L0_attn_Wq, L0_attn_Wk)
    h = h + _L0_ffn_ref(_layernorm(h, axis=-1), L0_ffn_gate_w, L0_ffn_gate_b, L0_ffn_w1, L0_ffn_b1, L0_ffn_w2, L0_ffn_b2, L0_ffn_gamma, L0_ffn_beta)
    return h

_drawn_inputs = setup_inputs


def setup_inputs(seed=0):
    import zlib

    import numpy as np

    out = dict(_drawn_inputs(seed))
    spreads = {'L0_ffn_gate_b': (0.0, 0.482),
     'L0_ffn_b1': (0.0, 0.8),
     'L0_ffn_b2': (0.0, 0.492),
     'L0_ffn_gamma': (1.0, 0.2),
     'L0_ffn_beta': (0.0, 0.322)}
    factors = {'L0_ffn_gate_w': 3.7, 'L0_ffn_w1': 8.0, 'L0_ffn_w2': 8.0}
    for name, (base, spread) in spreads.items():
        noise = np.random.default_rng([zlib.crc32(name.encode()), seed]).standard_normal(out[name].shape)
        drawn = base * np.exp(spread * noise) if base else spread * noise
        out[name] = jnp.asarray(drawn.astype(out[name].dtype))
    for name, factor in factors.items():
        out[name] = (out[name] * factor).astype(out[name].dtype)
    return out
```

```python
import math
from contextlib import ExitStack

import concourse.bass as bass
from concourse import mybir

F32 = mybir.dt.float32
F32R = mybir.dt.float32r
U32 = mybir.dt.uint32
ALU = mybir.AluOpType
ACT = mybir.ActivationFunctionType
AX = mybir.AxisListType

BATCH, S_IN, D, TAPS = 8, 750, 64, 16
TOK = S_IN - TAPS + 1
HALF = (TOK + 1) // 2
TOKP = 2 * HALF
P = 128
BLOCKS = -(-HALF // P)
NT = 2 * BLOCKS
LAST = HALF - (BLOCKS - 1) * P
FULL = NT - 2
CHUNKS = TAPS // 2
XT_TILES = -(-S_IN // P)
XT_LAST = S_IN - (XT_TILES - 1) * P
E, F = 16, 128
EPS = 1e-5
BANK = 512
ROUND = 1.5 * 2.0 ** 23
TWO_PI_HI = 6.28125
TWO_PI_LO = 2 * math.pi - TWO_PI_HI
PI_BELOW = 3.1415925
CONST = 11
MOE_LOADS = 10
CREDIT = 1


def tile_start(t):
    return (t % 2) * HALF + (t // 2) * P


def tile_size(t):
    return P if t < FULL else LAST


def key_size(t):
    return tile_size(t) - (1 if tile_start(t) + tile_size(t) > TOK else 0)


def row_of(rows, e):
    p = 32 * (e // 4)
    return rows[p:p + 1, e % 4, :]


def along(ap, shape):
    return ap.unsqueeze(2).broadcast_to(shape)


def build(nc, x, w_real, w_imag, phases, wq, wk, gate_w, gate_b, w1, b1, w2, b2, gamma, beta, out):
    ctx = ExitStack()
    with ctx:
        def sb(name, shape, dt=F32):
            return ctx.enter_context(nc.sbuf_tensor(name, shape, dt))

        def ps(name, shape):
            return ctx.enter_context(nc.psum_tensor(name, shape, F32))

        def sem(name):
            return ctx.enter_context(nc.semaphore(name))

        ident = sb("ident", [P, P])
        iota = sb("iota", [P, E])
        phase = sb("phase", [D, TAPS])
        trig = sb("trig", [D, 6, TAPS])
        wr = sb("wr", [D, D * TAPS])
        wi = sb("wi", [D, D * TAPS])
        w_eff = sb("w_eff", [D, TAPS, D])
        w_sin = sb("w_sin", [D, TAPS, D])
        conv_w = sb("conv_w", [P, CHUNKS, D])
        wq2 = sb("wq2", [D, 2, D])
        wk2 = sb("wk2", [D, 2, D])
        a_hi = sb("a_hi", [P, P], F32R)
        a_lo = sb("a_lo", [P, P], F32R)
        w1_raw = sb("w1_raw", [P, E, F])
        w1_hi = sb("w1_hi", [P, E, F], F32R)
        w1_lo = sb("w1_lo", [P, E, F], F32R)
        w2s = sb("w2s", [P, E, D])
        b1_rows = sb("b1_rows", [E, F])
        b1_neg = sb("b1_neg", [P, E])
        b1_diag = sb("b1_diag", [P, E, E])
        b2s = sb("b2s", [E, D])
        bias_w = sb("bias_w", [E, D])
        gw_raw = sb("gw_raw", [P, E])
        gw_hi = sb("gw_hi", [P, E], F32R)
        gw_lo = sb("gw_lo", [P, E], F32R)
        gb = sb("gb", [P, E])
        gam = sb("gam", [P, D])
        bet = sb("bet", [P, D])
        power = sb("power", [P, NT])

        xx = sb("xx", [P, XT_TILES, 2 * D])
        xt = sb("xt", [P, S_IN])
        conv_t = sb("conv_t", [P, HALF])
        h0 = sb("h0", [P, NT, D])
        xn1 = sb("xn1", [P, NT, 2 * D + 1])
        keys = sb("keys", [P, TOKP], F32R)
        keys1 = sb("keys1", [D + 1, TOKP], F32R)
        q_hi = sb("q_hi", [P, TOKP], F32R)
        q_lo = sb("q_lo", [D + 1, TOKP], F32R)
        row_max = sb("row_max", [P, NT, D + 1])
        probs = sb("probs", [P, NT, TOKP])
        rden = sb("rden", [P, NT])
        attn = sb("attn", [P, NT, D])
        h1 = [sb(f"h1_{k}", [P, NT, D]) for k in range(2)]
        xn2 = [sb(f"xn2_{k}", [P, NT, 2 * D]) for k in range(2)]
        x2 = [sb(f"x2_{k}", [P, TOKP], F32R) for k in range(2)]
        logits = sb("logits", [P, NT, E])
        top = sb("top", [P, NT, 8])
        top_at = sb("top_at", [P, NT, 8], U32)
        at = sb("at", [P, NT, 2])
        gap = sb("gap", [P, NT])
        expgap = sb("expgap", [P, NT])
        wsum = sb("wsum", [P, NT])
        wtop = sb("wtop", [P, 2, NT])
        pick = sb("pick", [P, 2, NT, E])
        gates = sb("gates", [P, NT, E])
        gates_t = sb("gates_t", [E, TOKP])
        gates_row = sb("gates_row", [P, E // 4, TOKP])
        gates_all = sb("gates_all", [P, E, TOKP])
        hidden = sb("hidden", [P, 2, 2, HALF])
        moe_t = sb("moe_t", [P, HALF])
        y = sb("y", [P, NT, D])
        res = [sb(f"res{k}", [P, NT, D]) for k in range(3)]
        outs = sb("outs", [P, NT, D])
        lsum = [sb(f"lsum{k}", [P, NT]) for k in range(3)]
        lcen = [sb(f"lcen{k}", [P, NT, D]) for k in range(3)]
        lsq = [sb(f"lsq{k}", [P, NT, D]) for k in range(3)]
        lsqs = [sb(f"lsqs{k}", [P, NT]) for k in range(3)]
        lvar = [sb(f"lvar{k}", [P, NT]) for k in range(3)]
        lstd = [sb(f"lstd{k}", [P, NT]) for k in range(3)]

        wide = [ps(f"wide{k}", [P, 2, BANK]) for k in range(2)]
        small = ps("small", [P, BANK])
        up = [ps(f"up{k}", [P, BANK]) for k in range(2)]
        mix = ps("mix", [P, BANK])

        s_conv_in = sem("conv_w_loaded")
        s_wqk_in = sem("wqk_loaded")
        s_moe_in = sem("moe_w_loaded")
        s_const = sem("constants_made")
        s_zero = sem("zeros_made")
        s_trig = sem("trig_steps")
        s_sin = sem("sin_done")
        s_weff = sem("w_eff_steps")
        s_wt = sem("conv_w_transposed")
        s_wc = sem("conv_w_ready")
        s_a = sem("a_product")
        s_ahi = sem("a_hi_ready")
        s_alo = sem("a_lo_ready")
        s_w1hi = sem("w1_hi_ready")
        s_w1lo = sem("w1_lo_ready")
        s_b1t = sem("b1_transposed")
        s_b1 = sem("b1_ready")
        s_bias = sem("bias_product")
        s_biasw = sem("bias_w_ready")
        s_x = sem("x_loaded")
        s_xt = sem("x_transposed")
        s_xtc = sem("xt_copied")
        s_conv = sem("conv_done")
        s_convc = sem("conv_copied")
        s_ht = sem("h_transposed")
        s_h0 = sem("h0_copied")
        s_lsum = [sem(f"ln{k}_sum") for k in range(3)]
        s_lcen = [sem(f"ln{k}_centred") for k in range(3)]
        s_lsq = [sem(f"ln{k}_squared") for k in range(3)]
        s_lsqs = [sem(f"ln{k}_square_sum") for k in range(3)]
        s_lvar = [sem(f"ln{k}_variance") for k in range(3)]
        s_lstd = [sem(f"ln{k}_rstd") for k in range(3)]
        s_ln = [sem(f"ln{k}_normed") for k in range(3)]
        s_t1 = sem("xn1_transposed")
        s_khi = sem("keys_hi_ready")
        s_klo = sem("keys_lo_ready")
        s_q = sem("q_product")
        s_qhi = sem("q_hi_ready")
        s_qlo = sem("q_lo_ready")
        s_rough = sem("max_scores_ready")
        s_max = sem("max_reduced")
        s_maxt = sem("max_transposed")
        s_shift = sem("shift_ready")
        s_score = sem("scores_ready")
        s_prob = sem("probs_ready")
        s_pv = sem("attention_summed")
        s_rden = sem("denominator_inverted")
        s_attn = sem("attention_scaled")
        s_h1 = sem("h1_ready")
        s_t2 = sem("xn2_transposed")
        s_x2hi = sem("x2_hi_ready")
        s_x2lo = sem("x2_lo_ready")
        s_lg = sem("logits_product")
        s_logit = sem("logits_ready")
        s_top = sem("top_values")
        s_topi = sem("top_indices")
        s_gap = sem("gap_ready")
        s_egap = sem("exp_gap_ready")
        s_gate = sem("gate_steps")
        s_gates = sem("gates_ready")
        s_gt = sem("gates_transposed")
        s_gtc = sem("gates_copied")
        s_flat = sem("gates_flattened")
        s_pace = sem("broadcast_paced")
        s_gall = sem("gates_broadcast")
        s_bmm = sem("bias_added")
        s_up = sem("up_ready")
        s_hid = sem("hidden_ready")
        s_down = sem("down_done")
        s_mixc = sem("mix_copied")
        s_ft = sem("mix_transposed")
        s_y = sem("y_ready")
        s_fin = sem("final_steps")
        s_res = sem("result_ready")
        s_out = sem("stored")

        block = ctx.enter_context(nc.Block())

        def pipeline(eng, iteration):
            iteration(0, 0, False, True, True)
            with eng.Fori(0, (BATCH - 2) // 2) as k:
                iteration(2 * k + 1, 1, True, True, True)
                iteration(2 * k + 2, 0, True, True, True)
            iteration(BATCH - 1, 1, True, True, False)
            iteration(BATCH, 0, True, False, False)

        def split(ap):
            return ap.rearrange("p (s n) -> p s n", s=2)

        @block.sync
        def _(sp):
            def load_x(b):
                rows = (XT_TILES - 1) * P
                flat = x[b].rearrange("t c -> (t c)")
                for h in range(2):
                    sp.dma_start(xx[:, 0:XT_TILES - 1, h * D:(h + 1) * D],
                                 flat[h * D:h * D + rows * D].rearrange("(i p c) -> p i c", p=P, c=D)
                                 ).then_inc(s_x, 16)
                    n = XT_LAST - h
                    sp.dma_start(xx[0:n, XT_TILES - 1, h * D:(h + 1) * D],
                                 flat[(rows + h) * D:(rows + h + n) * D].rearrange("(p c) -> p c", c=D)
                                 ).then_inc(s_x, 16)

            sp.sem_inc(s_out, 16 * CREDIT)
            sp.dma_start(phase[:], phases.partition_broadcast(D)).then_inc(s_conv_in, 16)
            sp.dma_start(wr[:], w_real.rearrange("o i k -> o (i k)")).then_inc(s_conv_in, 16)
            sp.dma_start(wi[:], w_imag.rearrange("o i k -> o (i k)")).then_inc(s_conv_in, 16)
            sp.wait_ge(s_zero, 1)
            load_x(0)
            for h in range(2):
                sp.dma_start(wq2[:, h, :], wq).then_inc(s_wqk_in, 16)
                sp.dma_start(wk2[:, h, :], wk).then_inc(s_wqk_in, 16)
            for h in range(2):
                sp.dma_start(gw_raw[h * D:(h + 1) * D, :], gate_w).then_inc(s_moe_in, 16)
                sp.dma_start(w1_raw[h * D:(h + 1) * D, :, :], w1.rearrange("e h f -> h e f")).then_inc(s_moe_in, 16)
            sp.dma_start(w2s[:], w2.rearrange("e f h -> f e h")).then_inc(s_moe_in, 16)
            sp.dma_start(b1_rows[:], b1).then_inc(s_moe_in, 16)
            sp.dma_start(b2s[:], b2).then_inc(s_moe_in, 16)
            sp.dma_start(gb[:], gate_b.partition_broadcast(P)).then_inc(s_moe_in, 16)
            sp.dma_start(gam[:], gamma.partition_broadcast(P)).then_inc(s_moe_in, 16)
            sp.dma_start(bet[:], beta.partition_broadcast(P)).then_inc(s_moe_in, 16)

            def store(b):
                sp.wait_ge(s_conv_in, 48)
                sp.wait_ge(s_res, CREDIT + b + 1)
                for h in range(2):
                    sp.dma_start(out[b, h * HALF:h * HALF + (BLOCKS - 1) * P, :].rearrange("(j p) c -> p j c", p=P),
                                 outs[:, h:FULL:2, :]).then_inc(s_out, 16)
                for t in range(FULL, NT):
                    sp.dma_start(out[b, tile_start(t):tile_start(t) + key_size(t), :],
                                 outs[0:key_size(t), t, :]).then_inc(s_out, 16)

            def iteration(i, par, moe, att, conv):
                if conv:
                    sp.wait_ge(s_conv_in, 48)
                    sp.wait_ge(s_xt, i + 1)
                    load_x(i + 1)
                if att:
                    sp.wait_ge(s_conv_in, 48)
                    sp.wait_ge(s_gtc, i + 1)
                    sp.wait_ge(s_gall, E * i)
                    for e in range(E):
                        sp.dma_start(row_of(gates_row, e), gates_t[e:e + 1, :]).then_inc(s_flat, 16)
                if moe:
                    store(i - 1)

            pipeline(sp, iteration)
            sp.wait_ge(s_out, 16 * CREDIT + 64 * BATCH)

        @block.gpsimd
        def _(pool):
            pool.sem_inc(s_res, CREDIT)
            pool.memset(xx[:, XT_TILES - 1, :], 0.0).then_inc(s_zero, 1)
            pool.memset(ident[:], 0.0).then_inc(s_zero, 1)
            pool.iota(iota[:], [[1, E]], base=0, channel_multiplier=0,
                      allow_small_or_imprecise_dtypes=True).then_inc(s_const, 1)
            pool.wait_ge(s_zero, 2)
            pool.affine_select(out=ident[:], in_=ident[:], compare_op=ALU.not_equal, fill=1.0,
                               base=0, pattern=[[-1, P]], channel_multiplier=1).then_inc(s_const, 1)
            pool.memset(power[:], -0.5).then_inc(s_const, 1)
            for t in (h0, row_max, attn, logits, y):
                pool.memset(t[:], 0.0).then_inc(s_const, 1)
            pool.memset(xn1[:, :, 2 * D:2 * D + 1], 1.0).then_inc(s_const, 1)
            pool.memset(b1_diag[:], 0.0).then_inc(s_const, 1)
            pool.wait_ge(s_const, CONST - 1)
            pool.memset(keys1[D:D + 1, :].bitcast(F32), 1.0).then_inc(s_const, 1)
            pool.wait_ge(s_const, CONST)

            def rstd(k, n):
                pool.wait_ge(s_lvar[k], n + 1)
                pool.tensor_tensor(lstd[k][:], lvar[k][:], power[:], ALU.pow).then_inc(s_lstd[k], 1)

            def iteration(i, par, moe, att, conv):
                if att:
                    rstd(1, i)
                if conv:
                    rstd(0, i + 1)

                def broadcast(e):
                    if moe:
                        pool.wait_ge(s_hid, 2 * E * (i - 1) + 2 * e + 2)
                    if e > 0:
                        pool.wait_ge(s_gall, E * i + e)
                    if moe or e > 0:
                        pool.sem_inc(s_pace, 1)
                    pool.partition_broadcast(gates_all[:, e, :], row_of(gates_row, e), P).then_inc(s_gall, 1)

                if att:
                    pool.wait_ge(s_flat, 16 * E * (i + 1))
                    pool.sem_inc(s_pace, 1)
                    for e in range(4):
                        broadcast(e)
                    pool.wait_ge(s_gall, E * i + 4)
                if moe:
                    m = i - 1
                    rstd(2, m)
                    pool.wait_ge(s_lstd[2], m + 1)
                    pool.tensor_tensor(res[0][:], lcen[2][:], along(lstd[2][:], [P, NT, D]), ALU.mult).then_inc(s_fin, 1)
                    pool.wait_ge(s_fin, 3 * m + 1)
                    pool.tensor_tensor(res[1][:], res[0][:], gam[:].unsqueeze(1).broadcast_to([P, NT, D]), ALU.mult).then_inc(s_fin, 1)
                    pool.wait_ge(s_fin, 3 * m + 2)
                    pool.tensor_tensor(res[2][:], res[1][:], bet[:].unsqueeze(1).broadcast_to([P, NT, D]), ALU.add).then_inc(s_fin, 1)
                    pool.wait_ge(s_fin, 3 * m + 3)
                    pool.wait_ge(s_out, 16 * CREDIT + 64 * m)
                    pool.tensor_tensor(outs[:], res[2][:], h1[1 - par][:], ALU.add).then_inc(s_res, 1)
                if att:
                    if moe:
                        pool.wait_ge(s_res, CREDIT + i)
                    for e in range(4, E):
                        broadcast(e)
                    pool.wait_ge(s_gall, E * (i + 1))

            rstd(0, 0)
            pipeline(pool, iteration)

        @block.scalar
        def _(act):
            def copy(dst, src, scale=1.0):
                return act.activation(dst, src, ACT.Copy, scale=scale)

            act.sem_inc(s_mixc, CREDIT)
            act.wait_ge(s_trig, 6)
            act.activation(trig[:, 5, :], trig[:, 3, :], ACT.Sin).then_inc(s_sin, 1)
            act.wait_ge(s_trig, 8)
            act.activation(trig[:, 4, :], trig[:, 1, :], ACT.Sin).then_inc(s_sin, 1)
            act.wait_ge(s_wt, 1)
            copy(conv_w[:].rearrange("p k o -> p (k o)"), small[:]).then_inc(s_wc, 1)

            def xt_copy(n):
                act.wait_ge(s_xt, n + 1)
                act.wait_ge(s_conv, n)
                copy(xt[:, 0:BANK], wide[1][:, 0, :])
                copy(xt[:, BANK:S_IN], wide[1][:, 1, 0:S_IN - BANK]).then_inc(s_xtc, 1)

            def conv_copy(n):
                act.wait_ge(s_conv, n + 1)
                act.wait_ge(s_ht, n)
                copy(conv_t[:], small[:, 0:HALF]).then_inc(s_convc, 1)

            def h0_copy(n):
                act.wait_ge(s_ht, n + 1)
                act.wait_ge(s_h1, n)
                copy(h0[:, 0:FULL, :], wide[0][:, 0, 0:FULL * D].rearrange("p (t c) -> p t c", c=D))
                copy(h0[0:LAST, FULL:NT, :],
                     wide[0][0:LAST, 0, FULL * D:NT * D].rearrange("p (t c) -> p t c", c=D)).then_inc(s_h0, 1)

            def square(k, n):
                act.wait_ge(s_lcen[k], n + 1)
                act.wait_ge(s_lsqs[k], CREDIT + n)
                act.activation(lsq[k][:], lcen[k][:], ACT.Square).then_inc(s_lsq[k], 1)

            def keys_hi(n):
                act.wait_ge(s_t1, n + 1)
                act.wait_ge(s_prob, NT * n)
                copy(split(keys[:]), wide[1][:, :, 0:HALF]).then_inc(s_khi, 1)
                copy(split(keys1[0:D, :]), wide[1][0:D, :, 0:HALF]).then_inc(s_khi, 1)

            def query_hi(n):
                act.wait_ge(s_q, n + 1)
                copy(split(q_hi[:]), wide[0][:, :, 0:HALF]).then_inc(s_qhi, 1)

            act.wait_ge(s_a, 1)
            copy(a_hi[:], small[:, 0:P], D ** -0.5).then_inc(s_ahi, 1)
            xt_copy(0)
            conv_copy(0)
            h0_copy(0)
            act.wait_ge(s_moe_in, 16 * MOE_LOADS)
            copy(gw_hi[:], gw_raw[:]).then_inc(s_w1hi, 1)
            copy(w1_hi[:], w1_raw[:]).then_inc(s_w1hi, 1)
            square(0, 0)
            keys_hi(0)
            query_hi(0)

            def iteration(i, par, moe, att, conv):
                if att:
                    act.wait_ge(s_maxt, i + 1)
                    copy(split(q_lo[D:D + 1, :]), wide[1][D:D + 1, :, 0:HALF], -1.0).then_inc(s_shift, 1)
                    for t in range(NT):
                        act.wait_ge(s_score, NT * i + t + 1)
                        if t == 0:
                            act.wait_ge(s_pv, i)
                        w = key_size(t)
                        act.activation(split(probs[0:w, t, :]), wide[t % 2][0:w, :, 0:HALF], ACT.Exp).then_inc(s_prob, 1)
                if conv:
                    xt_copy(i + 1)
                if att:
                    square(1, i)
                if conv:
                    conv_copy(i + 1)
                if att:
                    act.wait_ge(s_t2, i + 1)
                    copy(split(x2[par][:]), wide[0][:, :, 0:HALF]).then_inc(s_x2hi, 1)
                if conv:
                    h0_copy(i + 1)
                    square(0, i + 1)
                if att:
                    act.wait_ge(s_gap, i + 1)
                    act.activation(expgap[:], gap[:], ACT.Exp).then_inc(s_egap, 1)
                if conv:
                    keys_hi(i + 1)
                if att:
                    act.wait_ge(s_gt, i + 1)
                    act.wait_ge(s_bmm, i)
                    act.wait_ge(s_flat, 16 * E * i)
                    copy(split(gates_t[:]), wide[0][0:E, :, 0:HALF]).then_inc(s_gtc, 1)
                if moe:
                    act.wait_ge(s_down, CREDIT + E * i)
                    act.wait_ge(s_ft, CREDIT + i - 1)
                    copy(moe_t[:], mix[:, 0:HALF]).then_inc(s_mixc, 1)
                if conv:
                    query_hi(i + 1)
                if moe:
                    square(2, i - 1)

            pipeline(act, iteration)

        @block.vector
        def _(dve):
            for s in (s_y, *s_lsqs):
                dve.sem_inc(s, CREDIT)
            dve.wait_ge(s_conv_in, 48)
            ph, turns, r, c = phase[:], trig[:, 0, :], trig[:, 1, :], trig[:, 3, :]

            def step(n, ins):
                ins.then_inc(s_trig, 1)
                dve.wait_ge(s_trig, n)

            step(1, dve.tensor_scalar(turns, ph, 1 / (2 * math.pi), ROUND, ALU.mult, ALU.add))
            step(2, dve.tensor_scalar(trig[:, 2, :], turns, -ROUND, None, ALU.add))
            step(3, dve.scalar_tensor_tensor(r, trig[:, 2, :], -TWO_PI_HI, ph, ALU.mult, ALU.add))
            step(4, dve.scalar_tensor_tensor(turns, trig[:, 2, :], -TWO_PI_LO, r, ALU.mult, ALU.add))
            step(5, dve.scalar_tensor_tensor(trig[:, 2, :], turns, -1.0, turns, ALU.mult, ALU.max))
            step(6, dve.tensor_scalar(c, trig[:, 2, :], -1.0, math.pi / 2, ALU.mult, ALU.add))
            step(7, dve.tensor_scalar(r, turns, PI_BELOW, -PI_BELOW, ALU.min, ALU.max))
            dve.tensor_scalar(trig[:, 0, :], c, 1.0, None, ALU.mult).then_inc(s_trig, 1)
            dve.wait_ge(s_sin, 2)
            dve.tensor_tensor(w_eff[:], wr[:].rearrange("o (i k) -> o k i", k=TAPS),
                              along(trig[:, 5, :], [D, TAPS, D]), ALU.mult).then_inc(s_weff, 1)
            dve.tensor_tensor(w_sin[:], wi[:].rearrange("o (i k) -> o k i", k=TAPS),
                              along(trig[:, 4, :], [D, TAPS, D]), ALU.mult).then_inc(s_weff, 1)
            dve.wait_ge(s_weff, 2)
            dve.tensor_tensor(w_eff[:], w_eff[:], w_sin[:], ALU.subtract).then_inc(s_weff, 1)
            dve.wait_ge(s_const, CONST)

            def low(dst, whole, high, scale=None):
                if scale is None:
                    return dve.tensor_tensor(dst, whole, high.bitcast(F32), ALU.subtract)
                return dve.scalar_tensor_tensor(dst, whole, scale, high.bitcast(F32), ALU.mult, ALU.subtract)

            def centre(k, src, n):
                dve.tensor_reduce(lsum[k][:], src, AX.X, ALU.add).then_inc(s_lsum[k], 1)
                dve.wait_ge(s_lsum[k], n + 1)
                if k == 2:
                    dve.wait_ge(s_res, CREDIT + n)
                dve.scalar_tensor_tensor(lcen[k][:], along(lsum[k][:], [P, NT, D]), -1.0 / D, src,
                                         ALU.mult, ALU.add).then_inc(s_lcen[k], 1)

            def variance(k, n):
                dve.wait_ge(s_lsq[k], n + 1)
                dve.tensor_reduce(lsqs[k][:], lsq[k][:], AX.X, ALU.add).then_inc(s_lsqs[k], 1)
                dve.wait_ge(s_lsqs[k], CREDIT + n + 1)
                dve.tensor_scalar(lvar[k][:], lsqs[k][:], 1.0 / D, EPS, ALU.mult, ALU.add).then_inc(s_lvar[k], 1)

            def normalise(k, dst, n):
                dve.wait_ge(s_lstd[k], n + 1)
                dve.tensor_tensor(dst[:, :, 0:2 * D].rearrange("p t (a c) -> p t a c", a=2),
                                  lcen[k][:].unsqueeze(2).broadcast_to([P, NT, 2, D]),
                                  lstd[k][:].unsqueeze(2).unsqueeze(3).broadcast_to([P, NT, 2, D]),
                                  ALU.mult).then_inc(s_ln[k], 1)

            def keys_lo(n):
                dve.wait_ge(s_khi, 2 * n + 1)
                low(split(keys[D:P, :]), wide[1][D:P, :, 0:HALF], split(keys[D:P, :])).then_inc(s_klo, 1)

            def query_lo(n):
                dve.wait_ge(s_qhi, n + 1)
                low(split(q_lo[0:D, :]), wide[0][0:D, :, 0:HALF], split(q_hi[0:D, :])).then_inc(s_qlo, 1)

            dve.wait_ge(s_ahi, 1)
            low(a_lo[:], small[:, 0:P], a_hi[:], D ** -0.5).then_inc(s_alo, 1)
            dve.wait_ge(s_h0, 1)
            centre(0, h0[:], 0)
            dve.wait_ge(s_w1hi, 2)
            low(gw_lo[:], gw_raw[:], gw_hi[:]).then_inc(s_w1lo, 1)
            low(w1_lo[:], w1_raw[:], w1_hi[:]).then_inc(s_w1lo, 1)
            variance(0, 0)
            dve.wait_ge(s_b1t, 1)
            dve.tensor_scalar(b1_neg[:], mix[:, 0:E], -1.0, None, ALU.mult).then_inc(s_b1, 1)
            dve.tensor_copy(b1_diag[:].rearrange("p a b -> p (a b)")[:, 0:E * E:E + 1], mix[:, 0:E]).then_inc(s_b1, 1)
            dve.wait_ge(s_bias, 1)
            dve.tensor_tensor(bias_w[:], mix[0:E, D:2 * D], b2s[:], ALU.add).then_inc(s_biasw, 1)
            normalise(0, xn1, 0)
            keys_lo(0)
            query_lo(0)

            def reduce_max(i, t):
                w = tile_size(t)
                dve.wait_ge(s_rough, NT * i + t + 1)
                dve.tensor_reduce(row_max[0:w, t, D:D + 1], wide[t % 2][0:w, :, 0:HALF], AX.XY,
                                  ALU.max).then_inc(s_max, 1)

            def scale_attention(i):
                o = small[:, 0:NT * (D + 1)].rearrange("p (t c) -> p t c", c=D + 1)
                dve.wait_ge(s_pv, i + 1)
                dve.reciprocal(rden[:, 0:FULL].unsqueeze(2), o[:, 0:FULL, D:D + 1]).then_inc(s_rden, 1)
                dve.reciprocal(rden[0:LAST, FULL:NT].unsqueeze(2), o[0:LAST, FULL:NT, D:D + 1]).then_inc(s_rden, 1)
                dve.wait_ge(s_rden, 2 * i + 2)
                dve.tensor_tensor(attn[:, 0:FULL, :], o[:, 0:FULL, 0:D],
                                  along(rden[:, 0:FULL], [P, FULL, D]), ALU.mult).then_inc(s_attn, 1)
                dve.tensor_tensor(attn[0:LAST, FULL:NT, :], o[0:LAST, FULL:NT, 0:D],
                                  along(rden[0:LAST, FULL:NT], [LAST, 2, D]), ALU.mult).then_inc(s_attn, 1)

            def residual(i, par):
                dve.wait_ge(s_attn, 2 * i + 2)
                dve.tensor_tensor(h1[par][:], attn[:], h0[:], ALU.add).then_inc(s_h1, 1)

            def top_two(i):
                dve.wait_ge(s_lg, i + 1)
                lg = wide[1][:, 0, 0:NT * E].rearrange("p (t e) -> p t e", e=E)
                dve.tensor_tensor(logits[:, 0:FULL, :], lg[:, 0:FULL, :],
                                  gb[:].unsqueeze(1).broadcast_to([P, FULL, E]), ALU.add).then_inc(s_logit, 1)
                dve.tensor_tensor(logits[0:LAST, FULL:NT, :], lg[0:LAST, FULL:NT, :],
                                  gb[0:LAST, :].unsqueeze(1).broadcast_to([LAST, 2, E]), ALU.add).then_inc(s_logit, 1)
                dve.wait_ge(s_const, CONST)
                dve.wait_ge(s_logit, 2 * i + 2)
                for t in range(NT):
                    dve.max(top[:, t, :], logits[:, t, :]).then_inc(s_top, 1)
                dve.wait_ge(s_top, NT * i + NT)
                dve.tensor_tensor(gap[:].unsqueeze(2), top[:, :, 1:2], top[:, :, 0:1], ALU.subtract).then_inc(s_gap, 1)
                for t in range(NT):
                    dve.max_index(top_at[:, t, :], top[:, t, :], logits[:, t, :]).then_inc(s_topi, 1)

            def gate(i):
                g = 8 * i
                dve.wait_ge(s_topi, NT * i + NT)
                dve.tensor_copy(at[:], top_at[:, :, 0:2]).then_inc(s_gate, 1)
                dve.wait_ge(s_egap, i + 1)
                dve.tensor_scalar(wsum[:], expgap[:], 1.0, None, ALU.add).then_inc(s_gate, 1)
                dve.wait_ge(s_gate, g + 2)
                dve.reciprocal(wtop[:, 0, :], wsum[:]).then_inc(s_gate, 1)
                for k in range(2):
                    dve.tensor_tensor(pick[:, k, :, :], iota[:].unsqueeze(1).broadcast_to([P, NT, E]),
                                      at[:, :, k:k + 1].broadcast_to([P, NT, E]), ALU.is_equal).then_inc(s_gate, 1)
                dve.wait_ge(s_gate, g + 5)
                dve.tensor_tensor(wtop[:, 1, :], expgap[:], wtop[:, 0, :], ALU.mult).then_inc(s_gate, 1)
                dve.wait_ge(s_gate, g + 6)
                for k in range(2):
                    dve.tensor_tensor(pick[:, k, :, :], pick[:, k, :, :], along(wtop[:, k, :], [P, NT, E]),
                                      ALU.mult).then_inc(s_gate, 1)
                dve.wait_ge(s_gate, g + 8)
                dve.tensor_tensor(gates[:], pick[:, 0, :, :], pick[:, 1, :, :], ALU.add).then_inc(s_gates, 1)

            def hide(n, e, s):
                dve.wait_ge(s_up, 2 * E * n + 2 * e + s + 1)
                if s == 0:
                    dve.wait_ge(s_gall, E * n + e + 1)
                    dve.wait_ge(s_down, CREDIT + E * n + max(e - 1, 0))
                dve.scalar_tensor_tensor(hidden[:, e % 2, s, :], up[s][:, 0:HALF], b1_neg[:, e:e + 1],
                                         gates_all[:, e, s * HALF:(s + 1) * HALF],
                                         ALU.max, ALU.mult).then_inc(s_hid, 1)

            def iteration(i, par, moe, att, conv):
                for e in range(E):
                    if moe:
                        hide(i - 1, e, 0)
                        hide(i - 1, e, 1)
                    if att and e < 3:
                        reduce_max(i, 2 * e)
                        reduce_max(i, 2 * e + 1)
                    if att and e == 9:
                        scale_attention(i)
                        residual(i, par)
                        dve.wait_ge(s_h1, i + 1)
                        centre(1, h1[par][:], i)
                    if att and e == 10:
                        variance(1, i)
                    if att and e == 11:
                        normalise(1, xn2[par], i)
                    if att and e == 12:
                        dve.wait_ge(s_x2hi, i + 1)
                        low(split(x2[par][D:P, :]), wide[0][D:P, :, 0:HALF], split(x2[par][D:P, :])).then_inc(s_x2lo, 1)
                    if conv and e == 13:
                        dve.wait_ge(s_h0, i + 2)
                        centre(0, h0[:], i + 1)
                    if conv and e == 14:
                        variance(0, i + 1)
                    if att and e == 14:
                        top_two(i)
                    if conv and e == 15:
                        normalise(0, xn1, i + 1)
                    if att and e == 15:
                        gate(i)
                if conv:
                    keys_lo(i + 1)
                    query_lo(i + 1)
                if moe:
                    m = i - 1
                    dve.wait_ge(s_ft, CREDIT + m + 1)
                    ft = wide[1][:, 0, 0:NT * D].rearrange("p (t c) -> p t c", c=D)
                    dve.tensor_tensor(y[:, 0:FULL, :], ft[:, 0:FULL, :], xn2[1 - par][:, 0:FULL, 0:D], ALU.add).then_inc(s_y, 1)
                    dve.tensor_tensor(y[0:LAST, FULL:NT, :], ft[0:LAST, FULL:NT, :],
                                      xn2[1 - par][0:LAST, FULL:NT, 0:D], ALU.add).then_inc(s_y, 1)
                    dve.wait_ge(s_y, CREDIT + 2 * m + 2)
                    centre(2, y[:], m)
                    variance(2, m)

            pipeline(dve, iteration)

        @block.tensor
        def _(pe):
            def mm(dst, lhsT, rhs, start, stop):
                return pe.matmul(dst, lhsT, rhs, start=start, stop=stop, skip_group_check=True)

            pe.sem_inc(s_ft, CREDIT)
            pe.sem_inc(s_down, CREDIT)
            pe.wait_ge(s_const, CONST)
            pe.wait_ge(s_weff, 3)
            for k in range(CHUNKS):
                last = pe.transpose(small[:, k * D:(k + 1) * D],
                                    w_eff[:, 2 * k:2 * k + 2, :].rearrange("o k i -> o (k i)"), ident[0:D, 0:D])
            last.then_inc(s_wt, 1)

            def transpose_x(n):
                pe.wait_ge(s_x, 64 * (n + 1))
                for t in range(XT_TILES):
                    w = P if t < XT_TILES - 1 else XT_LAST
                    c = t * P
                    last = pe.transpose(wide[1][:, c // BANK, c % BANK:c % BANK + w], xx[0:w, t, :], ident[0:w, 0:w])
                last.then_inc(s_xt, 1)

            def convolve(n, first, end):
                for k in range(first, end):
                    for s in range(2):
                        a = s * HALF + 2 * k
                        last = mm(small[s * D:(s + 1) * D, 0:HALF], conv_w[:, k, :], xt[:, a:a + HALF],
                                  k == 0, k == CHUNKS - 1)
                if end == CHUNKS:
                    last.then_inc(s_conv, 1)

            def to_tokens(dst, src, done):
                for j in range(BLOCKS):
                    w = tile_size(2 * j)
                    last = pe.transpose(dst[0:w, 0, j * P:(j + 1) * P], src[:, j * P:j * P + w], ident[:])
                last.then_inc(done, 1)

            def to_features(dst, src, done):
                for t in range(NT):
                    w, j = tile_size(t), t // 2
                    last = pe.transpose(dst[:, t % 2, j * P:j * P + w],
                                        src[0:w, t, 0:2 * D], ident[0:w, 0:w])
                last.then_inc(done, 1)

            def project(n):
                pe.wait_ge(s_khi, 2 * n + 2)
                pe.wait_ge(s_klo, n + 1)
                for s in range(2):
                    rhs = keys[:, s * HALF:(s + 1) * HALF]
                    mm(wide[0][:, s, 0:HALF], a_hi[:], rhs, True, False)
                    last = mm(wide[0][:, s, 0:HALF], a_lo[:], rhs, False, True)
                last.then_inc(s_q, 1)

            transpose_x(0)
            pe.wait_ge(s_wqk_in, 64)
            pe.wait_ge(s_wc, 1)
            mm(small[:, 0:P], wq2[:].rearrange("o a d -> o (a d)"), wk2[:].rearrange("o a d -> o (a d)"),
               True, True).then_inc(s_a, 1)
            pe.wait_ge(s_moe_in, 16 * MOE_LOADS)
            pe.transpose(mix[:, 0:E], b1_rows[:], ident[0:E, 0:E]).then_inc(s_b1t, 1)
            pe.wait_ge(s_ahi, 1)
            pe.wait_ge(s_alo, 1)
            pe.wait_ge(s_xtc, 1)
            convolve(0, 0, CHUNKS)
            pe.wait_ge(s_convc, 1)
            to_tokens(wide[0], conv_t, s_ht)
            pe.wait_ge(s_b1, 2)
            for e in range(E):
                last = mm(mix[0:E, D:2 * D], b1_diag[:, e, :], w2s[:, e, :], e == 0, e == E - 1)
            last.then_inc(s_bias, 1)
            pe.wait_ge(s_ln[0], 1)
            to_features(wide[1], xn1, s_t1)
            pe.wait_ge(s_h0, 1)
            project(0)

            def max_scores(i, t):
                if t == 0:
                    pe.wait_ge(s_qhi, i + 1)
                    pe.wait_ge(s_qlo, i + 1)
                elif t >= 2:
                    pe.wait_ge(s_max, NT * i + t - 1)
                a, w = tile_start(t), tile_size(t)
                lhs = q_hi[:, a:a + w]
                mm(wide[t % 2][0:w, 0, 0:HALF], lhs, keys[:, 0:HALF], True, True)
                mm(wide[t % 2][0:w, 1, 0:HALF], lhs, keys[:, TOK - HALF:TOK], True, True).then_inc(s_rough, 1)

            def transpose_max(i):
                pe.wait_ge(s_max, NT * i + NT)
                for t in range(NT):
                    w, j = tile_size(t), t // 2
                    last = pe.transpose(wide[1][0:D + 1, t % 2, j * P:j * P + w], row_max[0:w, t, :], ident[0:w, 0:w])
                last.then_inc(s_maxt, 1)

            def scores(i, t):
                if t == 0:
                    pe.wait_ge(s_shift, i + 1)
                elif t >= 2:
                    pe.wait_ge(s_prob, NT * i + t - 1)
                a, w = tile_start(t), key_size(t)
                for s in range(2):
                    cols = slice(s * HALF, (s + 1) * HALF)
                    mm(wide[t % 2][0:w, s, 0:HALF], keys[:, a:a + w], q_hi[:, cols], True, False)
                    last = mm(wide[t % 2][0:w, s, 0:HALF], keys1[:, a:a + w], q_lo[:, cols], False, True)
                last.then_inc(s_score, 1)

            def weigh_values(i, t):
                pe.wait_ge(s_prob, NT * i + t + 1)
                w = key_size(t)
                for u in range(NT):
                    a, n = tile_start(u), tile_size(u)
                    last = mm(small[0:n, u * (D + 1):(u + 1) * (D + 1)], probs[0:w, t, a:a + n], xn1[0:w, t, D:2 * D + 1],
                              t == 0 and u == 0, t == NT - 1)
                if t == NT - 1:
                    last.then_inc(s_pv, 1)

            def gate_logits(i, par):
                pe.wait_ge(s_x2lo, i + 1)
                pe.wait_ge(s_w1lo, 2)
                for t in range(NT):
                    a, w = tile_start(t), tile_size(t)
                    dst = wide[1][0:w, 0, t * E:(t + 1) * E]
                    mm(dst, x2[par][:, a:a + w], gw_hi[:], True, False)
                    last = mm(dst, x2[par][:, a:a + w], gw_lo[:], False, True)
                last.then_inc(s_lg, 1)

            def transpose_gates(i):
                pe.wait_ge(s_gates, i + 1)
                for t in range(NT):
                    w, j = tile_size(t), t // 2
                    last = pe.transpose(wide[0][0:E, t % 2, j * P:j * P + w], gates[0:w, t, :], ident[0:w, 0:w])
                last.then_inc(s_gt, 1)

            def gated_biases(n):
                pe.wait_ge(s_biasw, 1)
                pe.wait_ge(s_gtc, n + 1)
                pe.wait_ge(s_mixc, CREDIT + n)
                for s in range(2):
                    last = mm(mix[s * D:(s + 1) * D, 0:HALF], bias_w[:], gates_t[:, s * HALF:(s + 1) * HALF],
                              True, False)
                last.then_inc(s_bmm, 1)

            def first_layer(n, e, buf):
                for s in range(2):
                    if e > 0:
                        pe.wait_ge(s_hid, 2 * E * n + 2 * e + s - 1)
                    rhs = x2[buf][:, s * HALF:(s + 1) * HALF]
                    mm(up[s][:, 0:HALF], w1_hi[:, e, :], rhs, True, False)
                    mm(up[s][:, 0:HALF], w1_lo[:, e, :], rhs, False, True).then_inc(s_up, 1)

            def second_layer(n, e):
                pe.wait_ge(s_hid, 2 * E * n + 2 * e + 2)
                for s in range(2):
                    last = mm(mix[s * D:(s + 1) * D, 0:HALF], w2s[:, e, :], hidden[:, e % 2, s, :], False, e == E - 1)
                last.then_inc(s_down, 1)

            def iteration(i, par, moe, att, conv):
                for e in range(E):
                    if moe:
                        if e == 0:
                            gated_biases(i - 1)
                        first_layer(i - 1, e, 1 - par)
                        if e > 0:
                            second_layer(i - 1, e - 1)
                    if att and e < 3:
                        for t in (2 * e, 2 * e + 1):
                            if t == 1 and moe:
                                pe.wait_ge(s_y, CREDIT + 2 * (i - 1))
                            max_scores(i, t)
                    if att and e == 3:
                        transpose_max(i)
                    if att and 4 <= e < 7:
                        scores(i, 2 * (e - 4))
                        scores(i, 2 * (e - 4) + 1)
                    if att and 6 <= e < 9:
                        weigh_values(i, 2 * (e - 6))
                        weigh_values(i, 2 * (e - 6) + 1)
                    if conv and e == 7:
                        pe.wait_ge(s_prob, NT * i + NT)
                        transpose_x(i + 1)
                    if conv and e == 10:
                        pe.wait_ge(s_attn, 2 * i + 2)
                        pe.wait_ge(s_xtc, i + 2)
                        convolve(i + 1, 0, CHUNKS // 2)
                    if conv and e == 11:
                        convolve(i + 1, CHUNKS // 2, CHUNKS)
                    if att and e == 12:
                        pe.wait_ge(s_ln[1], i + 1)
                        to_features(wide[0], xn2[par], s_t2)
                    if conv and e == 13:
                        pe.wait_ge(s_convc, i + 2)
                        pe.wait_ge(s_x2lo, i + 1)
                        to_tokens(wide[0], conv_t, s_ht)
                    if att and e == 13:
                        gate_logits(i, par)
                if conv:
                    pe.wait_ge(s_ln[0], i + 2)
                    pe.wait_ge(s_logit, 2 * i + 2)
                    to_features(wide[1], xn1, s_t1)
                if moe:
                    second_layer(i - 1, E - 1)
                if att:
                    if conv:
                        pe.wait_ge(s_h0, i + 2)
                    transpose_gates(i)
                if conv:
                    pe.wait_ge(s_gtc, i + 1)
                    project(i + 1)
                if moe:
                    pe.wait_ge(s_mixc, CREDIT + i)
                    if conv:
                        pe.wait_ge(s_klo, i + 2)
                    to_tokens(wide[1], moe_t, s_ft)

            pipeline(pe, iteration)


INPUTS = ["x", "L0_tok_w_real", "L0_tok_w_imag", "L0_tok_phases", "L0_attn_Wq", "L0_attn_Wk", "L0_ffn_gate_w",
          "L0_ffn_gate_b", "L0_ffn_w1", "L0_ffn_b1", "L0_ffn_w2", "L0_ffn_b2", "L0_ffn_gamma", "L0_ffn_beta"]


def kernel(**inputs):
    import numpy as np
    import concourse.bacc as bacc
    from concourse.bass_utils import run_bass_kernel_spmd

    nc = bacc.Bacc("TRN2", target_bir_lowering=False, num_devices=1)
    arrays, args = {}, []
    for name in INPUTS:
        a = np.ascontiguousarray(inputs[name])
        arrays[name] = a
        args.append(nc.dram_tensor(name, a.shape, F32, kind="ExternalInput").ap())
    out = nc.dram_tensor("out", (BATCH, TOK, D), F32, kind="ExternalOutput").ap()
    build(nc, *args, out)
    r = run_bass_kernel_spmd(nc, [arrays], core_ids=[0])
    return r.results[0]["out"]
```

```python
import math
from contextlib import ExitStack

import concourse.bass as bass
from concourse import mybir

F32 = mybir.dt.float32
F32R = mybir.dt.float32r
U32 = mybir.dt.uint32
ALU = mybir.AluOpType
ACT = mybir.ActivationFunctionType
AX = mybir.AxisListType

BATCH, S_IN, D, TAPS = 8, 750, 64, 16
TOK = S_IN - TAPS + 1
HALF = (TOK + 1) // 2
TOKP = 2 * HALF
P = 128
BLOCKS = -(-HALF // P)
NT = 2 * BLOCKS
LAST = HALF - (BLOCKS - 1) * P
FULL = NT - 2
CHUNKS = TAPS // 2
XT_TILES = -(-S_IN // P)
XT_PART = XT_TILES // 2 * P
XT_LAST = S_IN - (XT_TILES - 1) * P
E, F = 16, 128
ROW_GATES = E // 4
SPREAD = 10
POOLED = (10, 12, 14)
AHEAD = 4
CONV_CUTS = (0, 3, 6, CHUNKS)
EPS = 1e-5
BANK = 512
ROUND = 1.5 * 2.0 ** 23
TWO_PI_HI = 6.28125
TWO_PI_LO = 2 * math.pi - TWO_PI_HI
PI_BELOW = 3.1415925
CONST = 13
MOE_LOADS = 10
CREDIT = 1


def tile_start(t):
    return (t % 2) * HALF + (t // 2) * P


def tile_size(t):
    return P if t < FULL else LAST


def key_size(t):
    return tile_size(t) - (1 if tile_start(t) + tile_size(t) > TOK else 0)


def row_of(rows, e):
    p = 32 * (e // ROW_GATES)
    return rows[p:p + 1, e % ROW_GATES, :]


def hidden_before(n, e, s, pooled):
    group = [k for k in range(E) if (k in POOLED) == pooled]
    return 2 * len(group) * n + 2 * sum(k < e for k in group) + (s + 1 if e in group else 0)


def along(ap, shape):
    return ap.unsqueeze(2).broadcast_to(shape)


def build(nc, x, w_real, w_imag, phases, wq, wk, gate_w, gate_b, w1, b1, w2, b2, gamma, beta, out):
    ctx = ExitStack()
    with ctx:
        def sb(name, shape, dt=F32):
            return ctx.enter_context(nc.sbuf_tensor(name, shape, dt))

        def ps(name, shape):
            return ctx.enter_context(nc.psum_tensor(name, shape, F32))

        def sem(name):
            return ctx.enter_context(nc.semaphore(name))

        ident = sb("ident", [P, P])
        iota = sb("iota", [P, E])
        phase = sb("phase", [D, TAPS])
        trig = sb("trig", [D, 6, TAPS])
        wr = sb("wr", [D, D * TAPS])
        wi = sb("wi", [D, D * TAPS])
        w_eff = sb("w_eff", [D, TAPS, D])
        w_sin = sb("w_sin", [D, TAPS, D])
        conv_w = sb("conv_w", [P, CHUNKS, D])
        wq2 = sb("wq2", [D, 2, D])
        wk2 = sb("wk2", [D, 2, D])
        a_hi = sb("a_hi", [P, P], F32R)
        a_lo = sb("a_lo", [P, P], F32R)
        w1_raw = sb("w1_raw", [P, E, F])
        w1_hi = sb("w1_hi", [P, E, F], F32R)
        w1_lo = sb("w1_lo", [P, E, F], F32R)
        w2_sum = sb("w2_sum", [P, E])
        w2s = sb("w2s", [P, E, D])
        b1_rows = sb("b1_rows", [E, F])
        b1_neg = sb("b1_neg", [P, E])
        b1_pos = sb("b1_pos", [P, E])
        b1_diag = sb("b1_diag", [P, E, E])
        b2_raw = sb("b2_raw", [E, D])
        b2_sum = sb("b2_sum", [E, 1])
        b2s = sb("b2s", [E, D])
        bias_w = sb("bias_w", [E, D])
        gw_raw = sb("gw_raw", [P, E])
        gw_hi = sb("gw_hi", [P, E], F32R)
        gw_lo = sb("gw_lo", [P, E], F32R)
        gb = sb("gb", [P, E])
        gam = sb("gam", [P, D])
        bet = sb("bet", [P, D])
        power = sb("power", [P, NT])

        xx = sb("xx", [P, XT_TILES, 2 * D])
        xt = sb("xt", [P, S_IN])
        conv_t = sb("conv_t", [P, HALF])
        h0 = [sb(f"h0_{k}", [P, NT, D]) for k in range(2)]
        xn1 = [sb(f"xn1_{k}", [P, NT, 2 * D + 1]) for k in range(2)]
        keys = sb("keys", [P, TOKP], F32R)
        keys1 = sb("keys1", [D + 1, TOKP], F32R)
        q_hi = sb("q_hi", [P, TOKP], F32R)
        q_lo = sb("q_lo", [D + 1, TOKP], F32R)
        row_max = sb("row_max", [P, NT, D + 1])
        probs = sb("probs", [P, NT, TOKP])
        rden = sb("rden", [P, NT])
        attn = sb("attn", [P, NT, D])
        h1 = [sb(f"h1_{k}", [P, NT, D]) for k in range(2)]
        xn2 = [sb(f"xn2_{k}", [P, NT, 2 * D]) for k in range(2)]
        x2 = [sb(f"x2_{k}", [P, TOKP], F32R) for k in range(2)]
        logits = sb("logits", [P, NT, E])
        top = sb("top", [P, NT, 8])
        top_at = sb("top_at", [P, NT, 8], U32)
        at = sb("at", [P, NT, 2])
        gap = sb("gap", [P, NT])
        expgap = sb("expgap", [P, NT])
        wsum = sb("wsum", [P, NT])
        wtop = sb("wtop", [P, 2, NT])
        pick = sb("pick", [P, 2, NT, E])
        gates = sb("gates", [P, NT, E])
        gates_t = sb("gates_t", [E, TOKP])
        gates_row = sb("gates_row", [P, ROW_GATES, TOKP])
        gates_all = sb("gates_all", [P, E, TOKP])
        relu = sb("relu", [P, 2, HALF])
        hidden = sb("hidden", [P, 2, 2, HALF])
        moe_t = sb("moe_t", [P, HALF])
        moe_tok = sb("moe_tok", [P, NT, D])
        res = [sb(f"res{k}", [P, NT, D]) for k in range(3)]
        outs = sb("outs", [P, NT, D])
        mean_sum = sb("mean_sum", [P, NT])
        cen0 = [sb(f"cen0_{k}", [P, NT, D]) for k in range(2)]
        cen1 = sb("cen1", [P, NT, D])
        cen2 = sb("cen2", [P, NT, D])
        cen_sq = [sb(f"cen_sq{k}", [P, NT, D]) for k in range(3)]
        var = [sb(f"var{k}", [P, NT]) for k in range(3)]
        var_eps = [sb(f"var_eps{k}", [P, NT]) for k in range(3)]
        rstd = [sb(f"rstd{k}", [P, NT]) for k in range(3)]

        wide = [ps(f"wide{k}", [P, 2, BANK]) for k in range(2)]
        small = ps("small", [P, BANK])
        up = [ps(f"up{k}", [P, BANK]) for k in range(2)]
        mix = ps("mix", [P, BANK])

        s_conv_in = sem("conv_w_loaded")
        s_wqk_in = sem("wqk_loaded")
        s_moe_in = sem("moe_w_loaded")
        s_const = sem("constants_made")
        s_zero = sem("zeros_made")
        s_trig = sem("trig_steps")
        s_sin = sem("sin_done")
        s_weff = sem("w_eff_steps")
        s_wt = sem("conv_w_transposed")
        s_wc = sem("conv_w_ready")
        s_a = sem("a_product")
        s_ahi = sem("a_hi_ready")
        s_alo = sem("a_lo_ready")
        s_w1hi = sem("w1_hi_ready")
        s_w1lo = sem("w1_lo_ready")
        s_b1t = sem("b1_transposed")
        s_b1 = sem("b1_ready")
        s_w2 = sem("w2_steps")
        s_bias = sem("bias_product")
        s_biasw = sem("bias_w_ready")
        s_x = sem("x_loaded")
        s_xt = sem("x_transposed")
        s_xtc = sem("xt_copied")
        s_conv = sem("conv_done")
        s_convc = sem("conv_copied")
        s_ht = sem("h_transposed")
        s_h0 = sem("h0_copied")
        s_mean = sem("mean_summed")
        s_cen = [sem(f"ln{k}_centred") for k in range(3)]
        s_var = [sem(f"ln{k}_variance") for k in range(3)]
        s_eps = [sem(f"ln{k}_eps_added") for k in range(3)]
        s_rstd = [sem(f"ln{k}_rstd") for k in range(3)]
        s_ln = [sem(f"ln{k}_normed") for k in range(2)]
        s_t1 = sem("xn1_transposed")
        s_khi = sem("keys_hi_ready")
        s_klo = sem("keys_lo_ready")
        s_q = sem("q_product")
        s_qhi = sem("q_hi_ready")
        s_qlo = sem("q_lo_ready")
        s_rough = sem("max_scores_ready")
        s_max = sem("max_reduced")
        s_maxt = sem("max_transposed")
        s_shift = sem("shift_ready")
        s_score = sem("scores_ready")
        s_prob = sem("probs_ready")
        s_pv = sem("attention_summed")
        s_rden = sem("denominator_inverted")
        s_attn = sem("attention_scaled")
        s_h1 = sem("h1_ready")
        s_t2 = sem("xn2_transposed")
        s_x2hi = sem("x2_hi_ready")
        s_x2lo = sem("x2_lo_ready")
        s_lg = sem("logits_product")
        s_logit = sem("logits_ready")
        s_top = sem("top_values")
        s_topi = sem("top_indices")
        s_gap = sem("gap_ready")
        s_egap = sem("exp_gap_ready")
        s_gate = sem("gate_steps")
        s_gates = sem("gates_ready")
        s_gt = sem("gates_transposed")
        s_gtc = sem("gates_copied")
        s_flat = sem("gates_flattened")
        s_pace = sem("broadcast_paced")
        s_gall = sem("gates_broadcast")
        s_bmm = sem("bias_added")
        s_up = sem("up_ready")
        s_hid = sem("hidden_ready")
        s_relu = sem("relu_done")
        s_phid = sem("pooled_hidden_ready")
        s_down = sem("down_done")
        s_mixc = sem("mix_copied")
        s_ft = sem("mix_transposed")
        s_ftc = sem("mix_tokens_copied")
        s_fin = sem("final_steps")
        s_res = sem("result_ready")
        s_out = sem("stored")

        block = ctx.enter_context(nc.Block())

        def pipeline(eng, iteration, peeled=1):
            for i in range(peeled):
                iteration(i, i % 2, i, True, True)
            pairs = (BATCH - 1 - peeled) // 2
            with eng.Fori(0, pairs) as k:
                for j in range(2):
                    iteration(2 * k + peeled + j, (peeled + j) % 2, peeled, True, True)
            for i in range(peeled + 2 * pairs, BATCH + 1):
                iteration(i, i % 2, peeled, i < BATCH, i < BATCH - 1)

        def split(ap):
            return ap.rearrange("p (s n) -> p s n", s=2)

        @block.sync
        def _(sp):
            def load_x(b):
                rows = (XT_TILES - 1) * P
                flat = x[b].rearrange("t c -> (t c)")
                for h in range(2):
                    sp.dma_start(xx[:, 0:XT_TILES - 1, h * D:(h + 1) * D],
                                 flat[h * D:h * D + rows * D].rearrange("(i p c) -> p i c", p=P, c=D)
                                 ).then_inc(s_x, 16)
                    n = XT_LAST - h
                    sp.dma_start(xx[0:n, XT_TILES - 1, h * D:(h + 1) * D],
                                 flat[(rows + h) * D:(rows + h + n) * D].rearrange("(p c) -> p c", c=D)
                                 ).then_inc(s_x, 16)

            sp.sem_inc(s_out, 16 * CREDIT)
            sp.dma_start(phase[:], phases.partition_broadcast(D)).then_inc(s_conv_in, 16)
            sp.dma_start(wr[:], w_real.rearrange("o i k -> o (i k)")).then_inc(s_conv_in, 16)
            sp.dma_start(wi[:], w_imag.rearrange("o i k -> o (i k)")).then_inc(s_conv_in, 16)
            sp.wait_ge(s_zero, 1)
            load_x(0)
            for h in range(2):
                sp.dma_start(wq2[:, h, :], wq).then_inc(s_wqk_in, 16)
                sp.dma_start(wk2[:, h, :], wk).then_inc(s_wqk_in, 16)
            for h in range(2):
                sp.dma_start(gw_raw[h * D:(h + 1) * D, :], gate_w).then_inc(s_moe_in, 16)
                sp.dma_start(w1_raw[h * D:(h + 1) * D, :, :], w1.rearrange("e h f -> h e f")).then_inc(s_moe_in, 16)
            sp.dma_start(w2s[:], w2.rearrange("e f h -> f e h")).then_inc(s_moe_in, 16)
            sp.dma_start(b1_rows[:], b1).then_inc(s_moe_in, 16)
            sp.dma_start(b2_raw[:], b2).then_inc(s_moe_in, 16)
            sp.dma_start(gb[:], gate_b.partition_broadcast(P)).then_inc(s_moe_in, 16)
            sp.dma_start(gam[:], gamma.partition_broadcast(P)).then_inc(s_moe_in, 16)
            sp.dma_start(bet[:], beta.partition_broadcast(P)).then_inc(s_moe_in, 16)

            def store(b):
                sp.wait_ge(s_conv_in, 48)
                sp.wait_ge(s_res, CREDIT + b + 1)
                for h in range(2):
                    sp.dma_start(out[b, h * HALF:h * HALF + (BLOCKS - 1) * P, :].rearrange("(j p) c -> p j c", p=P),
                                 outs[:, h:FULL:2, :]).then_inc(s_out, 16)
                for t in range(FULL, NT):
                    sp.dma_start(out[b, tile_start(t):tile_start(t) + key_size(t), :],
                                 outs[0:key_size(t), t, :]).then_inc(s_out, 16)

            def load_next(n):
                sp.wait_ge(s_conv_in, 48)
                sp.wait_ge(s_xt, 2 * n)
                load_x(n)

            for n in range(1, AHEAD):
                load_next(n)
            with sp.Fori(0, BATCH - AHEAD) as b:
                load_next(b + AHEAD)
                store(b)
            for b in range(BATCH - AHEAD, BATCH):
                store(b)
            sp.wait_ge(s_out, 16 * CREDIT + 64 * BATCH)

        @block.gpsimd
        def _(pool):
            pool.sem_inc(s_res, CREDIT)
            pool.sem_inc(s_cen[2], CREDIT)
            pool.sem_inc(s_phid, CREDIT)
            pool.memset(xx[:, XT_TILES - 1, :], 0.0).then_inc(s_zero, 1)
            pool.memset(ident[:], 0.0).then_inc(s_zero, 1)
            pool.iota(iota[:], [[1, E]], base=0, channel_multiplier=0,
                      allow_small_or_imprecise_dtypes=True).then_inc(s_const, 1)
            pool.wait_ge(s_zero, 2)
            pool.affine_select(out=ident[:], in_=ident[:], compare_op=ALU.not_equal, fill=1.0,
                               base=0, pattern=[[-1, P]], channel_multiplier=1).then_inc(s_const, 1)
            pool.memset(power[:], -0.5).then_inc(s_const, 1)
            for t in (*h0, row_max, attn, logits, moe_tok):
                pool.memset(t[:], 0.0).then_inc(s_const, 1)
            for t in xn1:
                pool.memset(t[:, :, 2 * D:2 * D + 1], 1.0).then_inc(s_const, 1)
            pool.memset(b1_diag[:], 0.0).then_inc(s_const, 1)
            pool.wait_ge(s_const, CONST - 1)
            pool.memset(keys1[D:D + 1, :].bitcast(F32), 1.0).then_inc(s_const, 1)
            pool.wait_ge(s_const, CONST)

            def deviation(k, n):
                pool.wait_ge(s_var[k], n + 1)
                pool.sem_inc(s_pace, 1)
                pool.tensor_scalar(var_eps[k][:], var[k][:], EPS, None, ALU.add).then_inc(s_eps[k], 1)
                pool.wait_ge(s_eps[k], n + 1)
                pool.tensor_tensor(rstd[k][:], var_eps[k][:], power[:], ALU.pow).then_inc(s_rstd[k], 1)

            def broadcast(n, e, again):
                if again:
                    pool.wait_ge(s_hid, hidden_before(n - 1, e, 1, False))
                if e > 0:
                    pool.wait_ge(s_gall, E * n + e)
                if again or e > 0:
                    pool.sem_inc(s_pace, 1)
                pool.partition_broadcast(gates_all[:, e, :], row_of(gates_row, e), P).then_inc(s_gall, 1)

            def gate_hidden(n, e):
                for s in range(2):
                    pool.wait_ge(s_relu, hidden_before(n, e, s, True))
                    if s == 0:
                        pool.wait_ge(s_down, CREDIT + E * n + e - 1)
                    pool.tensor_tensor(hidden[:, e % 2, s, :], relu[:, s, :],
                                       gates_all[:, e, s * HALF:(s + 1) * HALF], ALU.mult).then_inc(s_phid, 1)

            def gamma_beta(m, buf):
                pool.wait_ge(s_rstd[2], m + 1)
                pool.tensor_tensor(res[0][:], cen2[:], along(rstd[2][:], [P, NT, D]), ALU.mult).then_inc(s_fin, 1)
                pool.wait_ge(s_fin, 3 * m + 1)
                pool.tensor_tensor(res[1][:], res[0][:], gam[:].unsqueeze(1).broadcast_to([P, NT, D]), ALU.mult).then_inc(s_fin, 1)
                pool.wait_ge(s_fin, 3 * m + 2)
                pool.tensor_tensor(res[2][:], res[1][:], bet[:].unsqueeze(1).broadcast_to([P, NT, D]), ALU.add).then_inc(s_fin, 1)
                pool.wait_ge(s_fin, 3 * m + 3)
                pool.wait_ge(s_out, 16 * CREDIT + 64 * m)
                pool.tensor_tensor(outs[:], res[2][:], h1[buf][:], ALU.add).then_inc(s_res, 1)

            def iteration(i, par, moe, att, conv):
                if conv:
                    deviation(0, i + 1)
                    pool.wait_ge(s_rstd[0], i + 2)
                if moe:
                    for e in range(SPREAD, E):
                        broadcast(i - 1, e, False)
                    pool.wait_ge(s_gall, E * i)
                if att:
                    pool.wait_ge(s_attn, 2 * i + 2)
                    pool.tensor_tensor(h1[par][:], attn[:], h0[par][:], ALU.add).then_inc(s_h1, 1)
                    deviation(1, i)
                    pool.wait_ge(s_rstd[1], i + 1)
                if moe:
                    for e in POOLED:
                        gate_hidden(i - 1, e)
                    pool.wait_ge(s_phid, CREDIT + hidden_before(i, 0, -1, True))
                if att:
                    pool.wait_ge(s_flat, 64 * (i + 1))
                    pool.sem_inc(s_pace, 1)
                    for e in range(2):
                        broadcast(i, e, moe)
                    pool.wait_ge(s_gall, E * i + 2)
                if moe:
                    m = i - 1
                    pool.wait_ge(s_hid, hidden_before(i, 0, -1, False))
                    pool.wait_ge(s_ftc, CREDIT + m + 1)
                    pool.tensor_tensor(cen2[:], moe_tok[:], xn2[1 - par][:, :, 0:D], ALU.add).then_inc(s_cen[2], 1)
                if att:
                    if moe:
                        pool.wait_ge(s_cen[2], CREDIT + i)
                    for e in range(2, 4):
                        broadcast(i, e, False)
                    pool.wait_ge(s_gall, E * i + 4)
                if moe:
                    deviation(2, m)
                    gamma_beta(m, 1 - par)
                if att:
                    if moe:
                        pool.wait_ge(s_res, CREDIT + i)
                    for e in range(4, SPREAD):
                        broadcast(i, e, False)
                    pool.wait_ge(s_gall, E * i + SPREAD)

            deviation(0, 0)
            pipeline(pool, iteration)

        @block.scalar
        def _(act):
            def copy(dst, src, scale=1.0):
                return act.activation(dst, src, ACT.Copy, scale=scale)

            act.sem_inc(s_mixc, CREDIT)
            act.sem_inc(s_ftc, CREDIT)
            act.wait_ge(s_trig, 6)
            act.activation(trig[:, 5, :], trig[:, 3, :], ACT.Sin).then_inc(s_sin, 1)
            act.wait_ge(s_trig, 8)
            act.activation(trig[:, 4, :], trig[:, 1, :], ACT.Sin).then_inc(s_sin, 1)
            act.wait_ge(s_wt, 1)
            copy(conv_w[:].rearrange("p k o -> p (k o)"), small[:]).then_inc(s_wc, 1)

            def xt_copy(n, part):
                act.wait_ge(s_xt, 2 * n + part + 1)
                if part == 0:
                    act.wait_ge(s_conv, n)
                lo = part * XT_PART
                w = min(XT_PART, S_IN - lo)
                copy(xt[:, lo:lo + w], small[:, 0:w]).then_inc(s_xtc, 1)

            def conv_copy(n):
                act.wait_ge(s_conv, n + 1)
                act.wait_ge(s_ht, n)
                copy(conv_t[:], small[:, 0:HALF]).then_inc(s_convc, 1)

            def tokens_copy(dst, done):
                src = small[:, 0:NT * D].rearrange("p (t c) -> p t c", c=D)
                copy(dst[:, 0:FULL, :], src[:, 0:FULL, :])
                copy(dst[0:LAST, FULL:NT, :], src[0:LAST, FULL:NT, :]).then_inc(done, 1)

            def h0_copy(n, buf):
                act.wait_ge(s_ht, n + 1)
                tokens_copy(h0[buf], s_h0)

            def variance(k, src, n):
                act.wait_ge(s_cen[k], n + 1 + (CREDIT if k == 2 else 0))
                for t in range(NT):
                    last = act.activation(cen_sq[k][:, t, :], src[:, t, :], ACT.Square, scale=D ** -0.5,
                                          accum_out=var[k][:, t:t + 1])
                last.then_inc(s_var[k], 1)

            def keys_hi(n):
                act.wait_ge(s_t1, n + 1)
                act.wait_ge(s_prob, NT * n)
                copy(split(keys[:]), wide[1][:, :, 0:HALF]).then_inc(s_khi, 1)
                copy(split(keys1[0:D, :]), wide[1][0:D, :, 0:HALF]).then_inc(s_khi, 1)

            def query_hi(n):
                act.wait_ge(s_q, n + 1)
                copy(split(q_hi[:]), wide[0][:, :, 0:HALF]).then_inc(s_qhi, 1)

            xt_copy(0, 0)
            xt_copy(0, 1)
            act.wait_ge(s_a, 1)
            copy(a_hi[:], wide[0][:, 0, 0:P], D ** -0.5).then_inc(s_ahi, 1)
            conv_copy(0)
            h0_copy(0, 0)
            variance(0, cen0[0], 0)
            keys_hi(0)
            query_hi(0)
            act.wait_ge(s_moe_in, 16 * MOE_LOADS)
            copy(gw_hi[:], gw_raw[:]).then_inc(s_w1hi, 1)
            copy(w1_hi[:], w1_raw[:]).then_inc(s_w1hi, 1)

            def rectify(n, e):
                for s in range(2):
                    act.wait_ge(s_up, 2 * E * n + 2 * e + s + 1)
                    if s == 0:
                        act.wait_ge(s_phid, CREDIT + hidden_before(n, e, -1, True))
                    act.activation(relu[:, s, :], up[s][:, 0:HALF], ACT.Relu, bias=b1_pos[:, e:e + 1]).then_inc(s_relu, 1)

            def exponentials(i, first, end):
                for t in range(first, end):
                    act.wait_ge(s_score, NT * i + t + 1)
                    if t == 0:
                        act.wait_ge(s_pv, i)
                    w = key_size(t)
                    act.activation(split(probs[0:w, t, :]), wide[t % 2][0:w, :, 0:HALF], ACT.Exp).then_inc(s_prob, 1)

            def iteration(i, par, moe, att, conv):
                if conv:
                    xt_copy(i + 1, 0)
                    xt_copy(i + 1, 1)
                if moe > 1:
                    variance(2, cen2, i - 2)
                if att:
                    act.wait_ge(s_maxt, i + 1)
                    copy(split(q_lo[D:D + 1, :]), wide[1][D:D + 1, :, 0:HALF], -1.0).then_inc(s_shift, 1)
                    exponentials(i, 0, 4)
                if conv:
                    conv_copy(i + 1)
                if att:
                    exponentials(i, 4, NT)
                if conv:
                    h0_copy(i + 1, 1 - par)
                    variance(0, cen0[1 - par], i + 1)
                if att:
                    variance(1, cen1, i)
                if conv:
                    keys_hi(i + 1)
                if moe:
                    rectify(i - 1, 10)
                if conv:
                    query_hi(i + 1)
                if att:
                    act.wait_ge(s_t2, i + 1)
                    copy(split(x2[par][:]), wide[1][:, :, 0:HALF]).then_inc(s_x2hi, 1)
                if moe:
                    rectify(i - 1, 12)
                if att:
                    act.wait_ge(s_gap, i + 1)
                    act.activation(expgap[:], gap[:], ACT.Exp).then_inc(s_egap, 1)
                if moe:
                    rectify(i - 1, 14)
                if att:
                    act.wait_ge(s_gt, i + 1)
                    act.wait_ge(s_bmm, i)
                    act.wait_ge(s_flat, 64 * i)
                    copy(split(gates_t[:]), wide[0][0:E, :, 0:HALF]).then_inc(s_gtc, 1)
                    act.wait_ge(s_gtc, i + 1)
                    act.wait_ge(s_gall, E * i)
                    for g in range(E // ROW_GATES):
                        act.dma_start(gates_row[32 * g:32 * g + 1, :, :],
                                      gates_t[ROW_GATES * g:ROW_GATES * (g + 1), :]).then_inc(s_flat, 16)
                if moe:
                    act.wait_ge(s_down, CREDIT + E * i)
                    act.wait_ge(s_ft, CREDIT + i - 1)
                    copy(moe_t[:], mix[:, 0:HALF]).then_inc(s_mixc, 1)
                    act.wait_ge(s_ft, CREDIT + i)
                    act.wait_ge(s_cen[2], CREDIT + i - 1)
                    tokens_copy(moe_tok, s_ftc)

            pipeline(act, iteration, 2)
            variance(2, cen2, BATCH - 1)

        @block.vector
        def _(dve):
            dve.wait_ge(s_conv_in, 48)
            ph, turns, r, c = phase[:], trig[:, 0, :], trig[:, 1, :], trig[:, 3, :]

            def step(n, ins):
                ins.then_inc(s_trig, 1)
                dve.wait_ge(s_trig, n)

            step(1, dve.tensor_scalar(turns, ph, 1 / (2 * math.pi), ROUND, ALU.mult, ALU.add))
            step(2, dve.tensor_scalar(trig[:, 2, :], turns, -ROUND, None, ALU.add))
            step(3, dve.scalar_tensor_tensor(r, trig[:, 2, :], -TWO_PI_HI, ph, ALU.mult, ALU.add))
            step(4, dve.scalar_tensor_tensor(turns, trig[:, 2, :], -TWO_PI_LO, r, ALU.mult, ALU.add))
            step(5, dve.scalar_tensor_tensor(trig[:, 2, :], turns, -1.0, turns, ALU.mult, ALU.max))
            step(6, dve.tensor_scalar(c, trig[:, 2, :], -1.0, math.pi / 2, ALU.mult, ALU.add))
            step(7, dve.tensor_scalar(r, turns, PI_BELOW, -PI_BELOW, ALU.min, ALU.max))
            dve.tensor_scalar(trig[:, 0, :], c, 1.0, None, ALU.mult).then_inc(s_trig, 1)
            dve.wait_ge(s_sin, 2)
            dve.tensor_tensor(w_eff[:], wr[:].rearrange("o (i k) -> o k i", k=TAPS),
                              along(trig[:, 5, :], [D, TAPS, D]), ALU.mult).then_inc(s_weff, 1)
            dve.tensor_tensor(w_sin[:], wi[:].rearrange("o (i k) -> o k i", k=TAPS),
                              along(trig[:, 4, :], [D, TAPS, D]), ALU.mult).then_inc(s_weff, 1)
            dve.wait_ge(s_weff, 2)
            dve.tensor_tensor(w_eff[:], w_eff[:], w_sin[:], ALU.subtract).then_inc(s_weff, 1)
            dve.wait_ge(s_const, CONST)

            def low(dst, whole, high, scale=None):
                if scale is None:
                    return dve.tensor_tensor(dst, whole, high.bitcast(F32), ALU.subtract)
                return dve.scalar_tensor_tensor(dst, whole, scale, high.bitcast(F32), ALU.mult, ALU.subtract)

            def centre(n, buf):
                dve.wait_ge(s_h0, n + 1)
                dve.tensor_reduce(mean_sum[:], h0[buf][:], AX.X, ALU.add).then_inc(s_mean, 1)
                dve.wait_ge(s_mean, n + 1)
                dve.scalar_tensor_tensor(cen0[buf][:], along(mean_sum[:], [P, NT, D]), -1.0 / D, h0[buf][:],
                                         ALU.mult, ALU.add).then_inc(s_cen[0], 1)

            def normalise(k, dst, src, n):
                dve.wait_ge(s_rstd[k], n + 1)
                dve.tensor_tensor(dst[:, :, 0:2 * D].rearrange("p t (a c) -> p t a c", a=2),
                                  src[:].unsqueeze(2).broadcast_to([P, NT, 2, D]),
                                  rstd[k][:].unsqueeze(2).unsqueeze(3).broadcast_to([P, NT, 2, D]),
                                  ALU.mult).then_inc(s_ln[k], 1)

            def keys_lo(n):
                dve.wait_ge(s_khi, 2 * n + 1)
                low(split(keys[D:P, :]), wide[1][D:P, :, 0:HALF], split(keys[D:P, :])).then_inc(s_klo, 1)

            def query_lo(n):
                dve.wait_ge(s_qhi, n + 1)
                low(split(q_lo[0:D, :]), wide[0][0:D, :, 0:HALF], split(q_hi[0:D, :])).then_inc(s_qlo, 1)

            dve.wait_ge(s_ahi, 1)
            low(a_lo[:], wide[0][:, 0, 0:P], a_hi[:], D ** -0.5).then_inc(s_alo, 1)
            centre(0, 0)
            normalise(0, xn1[0], cen0[0], 0)
            keys_lo(0)
            query_lo(0)
            def mixture_weights():
                dve.wait_ge(s_w1hi, 2)
                low(gw_lo[:], gw_raw[:], gw_hi[:]).then_inc(s_w1lo, 1)
                low(w1_lo[:], w1_raw[:], w1_hi[:]).then_inc(s_w1lo, 1)
                dve.tensor_reduce(w2_sum[:], w2s[:], AX.X, ALU.add).then_inc(s_w2, 1)
                dve.tensor_reduce(b2_sum[:], b2_raw[:], AX.X, ALU.add).then_inc(s_w2, 1)
                dve.wait_ge(s_w2, 2)
                dve.scalar_tensor_tensor(w2s[:], along(w2_sum[:], [P, E, D]), -1.0 / D, w2s[:],
                                         ALU.mult, ALU.add).then_inc(s_w2, 1)
                dve.scalar_tensor_tensor(b2s[:], b2_sum[:].broadcast_to([E, D]), -1.0 / D, b2_raw[:],
                                         ALU.mult, ALU.add).then_inc(s_w2, 1)
                dve.wait_ge(s_b1t, 1)
                dve.tensor_scalar(b1_neg[:], mix[:, 0:E], -1.0, None, ALU.mult).then_inc(s_b1, 1)
                dve.tensor_copy(b1_pos[:], mix[:, 0:E]).then_inc(s_b1, 1)
                dve.tensor_copy(b1_diag[:].rearrange("p a b -> p (a b)")[:, 0:E * E:E + 1], mix[:, 0:E]).then_inc(s_b1, 1)
                dve.wait_ge(s_w2, 4)

            def bias_weights():
                dve.wait_ge(s_bias, 1)
                dve.tensor_tensor(bias_w[:], mix[0:E, D:2 * D], b2s[:], ALU.add).then_inc(s_biasw, 1)

            def reduce_max(i, t):
                w = tile_size(t)
                dve.wait_ge(s_rough, NT * i + t + 1)
                dve.tensor_reduce(row_max[0:w, t, D:D + 1], wide[1 - t % 2][0:w, :, 0:HALF], AX.XY,
                                  ALU.max).then_inc(s_max, 1)

            def scale_attention(i):
                o = small[:, 0:NT * (D + 1)].rearrange("p (t c) -> p t c", c=D + 1)
                dve.wait_ge(s_pv, i + 1)
                dve.reciprocal(rden[:, 0:FULL].unsqueeze(2), o[:, 0:FULL, D:D + 1]).then_inc(s_rden, 1)
                dve.reciprocal(rden[0:LAST, FULL:NT].unsqueeze(2), o[0:LAST, FULL:NT, D:D + 1]).then_inc(s_rden, 1)
                dve.wait_ge(s_rden, 2 * i + 2)
                dve.tensor_tensor(attn[:, 0:FULL, :], o[:, 0:FULL, 0:D],
                                  along(rden[:, 0:FULL], [P, FULL, D]), ALU.mult).then_inc(s_attn, 1)
                dve.tensor_tensor(attn[0:LAST, FULL:NT, :], o[0:LAST, FULL:NT, 0:D],
                                  along(rden[0:LAST, FULL:NT], [LAST, 2, D]), ALU.mult).then_inc(s_attn, 1)

            def centre_sum(i, buf):
                dve.wait_ge(s_attn, 2 * i + 2)
                dve.tensor_tensor(cen1[:], attn[:], cen0[buf][:], ALU.add).then_inc(s_cen[1], 1)

            def top_two(i):
                dve.wait_ge(s_lg, i + 1)
                lg = small[:, 0:NT * E].rearrange("p (t e) -> p t e", e=E)
                dve.tensor_tensor(logits[:, 0:FULL, :], lg[:, 0:FULL, :],
                                  gb[:].unsqueeze(1).broadcast_to([P, FULL, E]), ALU.add).then_inc(s_logit, 1)
                dve.tensor_tensor(logits[0:LAST, FULL:NT, :], lg[0:LAST, FULL:NT, :],
                                  gb[0:LAST, :].unsqueeze(1).broadcast_to([LAST, 2, E]), ALU.add).then_inc(s_logit, 1)
                dve.wait_ge(s_const, CONST)
                dve.wait_ge(s_logit, 2 * i + 2)
                for t in range(NT):
                    dve.max(top[:, t, :], logits[:, t, :]).then_inc(s_top, 1)
                dve.wait_ge(s_top, NT * i + NT)
                dve.tensor_tensor(gap[:].unsqueeze(2), top[:, :, 1:2], top[:, :, 0:1], ALU.subtract).then_inc(s_gap, 1)
                for t in range(NT):
                    dve.max_index(top_at[:, t, :], top[:, t, :], logits[:, t, :]).then_inc(s_topi, 1)

            def gate(i):
                g = 8 * i
                dve.wait_ge(s_topi, NT * i + NT)
                dve.tensor_copy(at[:], top_at[:, :, 0:2]).then_inc(s_gate, 1)
                dve.wait_ge(s_egap, i + 1)
                dve.tensor_scalar(wsum[:], expgap[:], 1.0, None, ALU.add).then_inc(s_gate, 1)
                dve.wait_ge(s_gate, g + 2)
                dve.reciprocal(wtop[:, 0, :], wsum[:]).then_inc(s_gate, 1)
                for k in range(2):
                    dve.tensor_tensor(pick[:, k, :, :], iota[:].unsqueeze(1).broadcast_to([P, NT, E]),
                                      at[:, :, k:k + 1].broadcast_to([P, NT, E]), ALU.is_equal).then_inc(s_gate, 1)
                dve.wait_ge(s_gate, g + 5)
                dve.tensor_tensor(wtop[:, 1, :], expgap[:], wtop[:, 0, :], ALU.mult).then_inc(s_gate, 1)
                dve.wait_ge(s_gate, g + 6)
                for k in range(2):
                    dve.tensor_tensor(pick[:, k, :, :], pick[:, k, :, :], along(wtop[:, k, :], [P, NT, E]),
                                      ALU.mult).then_inc(s_gate, 1)
                dve.wait_ge(s_gate, g + 8)
                dve.tensor_tensor(gates[:], pick[:, 0, :, :], pick[:, 1, :, :], ALU.add).then_inc(s_gates, 1)

            def hide(n, e, s):
                dve.wait_ge(s_up, 2 * E * n + 2 * e + s + 1)
                if s == 0:
                    dve.wait_ge(s_gall, E * n + e + 1)
                    dve.wait_ge(s_down, CREDIT + E * n + max(e - 1, 0))
                dve.scalar_tensor_tensor(hidden[:, e % 2, s, :], up[s][:, 0:HALF], b1_neg[:, e:e + 1],
                                         gates_all[:, e, s * HALF:(s + 1) * HALF],
                                         ALU.max, ALU.mult).then_inc(s_hid, 1)

            def iteration(i, par, moe, att, conv):
                for e in range(E):
                    if moe and e not in POOLED:
                        hide(i - 1, e, 0)
                        hide(i - 1, e, 1)
                    if att and e == 0:
                        reduce_max(i, 4)
                        reduce_max(i, 5)
                    if not moe and e == 1:
                        mixture_weights()
                    if not moe and e == 11:
                        bias_weights()
                    if conv and e == 5:
                        centre(i + 1, 1 - par)
                    if conv and e == 7:
                        normalise(0, xn1[1 - par], cen0[1 - par], i + 1)
                    if att and e == 8:
                        scale_attention(i)
                        centre_sum(i, par)
                    if conv and e == 9:
                        keys_lo(i + 1)
                    if att and e == 10:
                        normalise(1, xn2[par], cen1, i)
                    if conv and e == 12:
                        query_lo(i + 1)
                    if att and e == 11:
                        dve.wait_ge(s_x2hi, i + 1)
                        low(split(x2[par][D:P, :]), wide[1][D:P, :, 0:HALF], split(x2[par][D:P, :])).then_inc(s_x2lo, 1)
                    if att and e == 12:
                        top_two(i)
                    if att and e == 13:
                        gate(i)
                if conv:
                    for t in range(4):
                        reduce_max(i + 1, t)

            for t in range(4):
                reduce_max(0, t)
            pipeline(dve, iteration)

        @block.tensor
        def _(pe):
            def mm(dst, lhsT, rhs, start, stop):
                return pe.matmul(dst, lhsT, rhs, start=start, stop=stop, skip_group_check=True)

            pe.sem_inc(s_ft, CREDIT)
            pe.sem_inc(s_down, CREDIT)
            pe.wait_ge(s_const, CONST)
            pe.wait_ge(s_weff, 3)
            for k in range(CHUNKS):
                last = pe.transpose(small[:, k * D:(k + 1) * D],
                                    w_eff[:, 2 * k:2 * k + 2, :].rearrange("o k i -> o (k i)"), ident[0:D, 0:D])
            last.then_inc(s_wt, 1)

            def transpose_x(n, part):
                if part == 0:
                    pe.wait_ge(s_x, 64 * (n + 1))
                else:
                    pe.wait_ge(s_xtc, 2 * n + 1)
                lo = part * XT_TILES // 2
                for t in range(lo, lo + XT_TILES // 2):
                    w = P if t < XT_TILES - 1 else XT_LAST
                    last = pe.transpose(small[:, (t - lo) * P:(t - lo) * P + w], xx[0:w, t, :], ident[0:w, 0:w])
                last.then_inc(s_xt, 1)

            def convolve(n, first, end):
                if first == 0:
                    pe.wait_ge(s_xtc, 2 * n + 2)
                for k in range(first, end):
                    for s in range(2):
                        a = s * HALF + 2 * k
                        last = mm(small[s * D:(s + 1) * D, 0:HALF], conv_w[:, k, :], xt[:, a:a + HALF],
                                  k == 0, k == CHUNKS - 1)
                if end == CHUNKS:
                    last.then_inc(s_conv, 1)

            def to_tokens(src, done):
                for j in range(BLOCKS):
                    w = tile_size(2 * j)
                    last = pe.transpose(small[0:w, j * P:(j + 1) * P], src[:, j * P:j * P + w], ident[:])
                last.then_inc(done, 1)

            def to_features(dst, src, done):
                for t in range(NT):
                    w, j = tile_size(t), t // 2
                    last = pe.transpose(dst[:, t % 2, j * P:j * P + w],
                                        src[0:w, t, 0:2 * D], ident[0:w, 0:w])
                last.then_inc(done, 1)

            def project(n):
                pe.wait_ge(s_khi, 2 * n + 2)
                pe.wait_ge(s_klo, n + 1)
                for s in range(2):
                    rhs = keys[:, s * HALF:(s + 1) * HALF]
                    mm(wide[0][:, s, 0:HALF], a_hi[:], rhs, True, False)
                    last = mm(wide[0][:, s, 0:HALF], a_lo[:], rhs, False, True)
                last.then_inc(s_q, 1)

            pe.wait_ge(s_wc, 1)
            transpose_x(0, 0)
            transpose_x(0, 1)
            pe.wait_ge(s_wqk_in, 64)
            mm(wide[0][:, 0, 0:P], wq2[:].rearrange("o a d -> o (a d)"), wk2[:].rearrange("o a d -> o (a d)"),
               True, True).then_inc(s_a, 1)
            convolve(0, 0, CHUNKS)
            pe.wait_ge(s_convc, 1)
            to_tokens(conv_t, s_ht)
            pe.wait_ge(s_ln[0], 1)
            to_features(wide[1], xn1[0], s_t1)
            pe.wait_ge(s_ahi, 1)
            pe.wait_ge(s_alo, 1)
            project(0)

            def max_scores(i, t, again=True):
                buf = 1 - t % 2
                if t == 0:
                    pe.wait_ge(s_qhi, i + 1)
                    pe.wait_ge(s_khi, 2 * i + 2)
                    pe.wait_ge(s_klo, i + 1)
                    if again:
                        pe.wait_ge(s_x2lo, i)
                elif t == 1:
                    pe.wait_ge(s_qlo, i + 1)
                    if again:
                        pe.wait_ge(s_gtc, i)
                elif t >= 2:
                    pe.wait_ge(s_max, NT * i + t - 1)
                a, w = tile_start(t), tile_size(t)
                lhs = q_hi[:, a:a + w]
                mm(wide[buf][0:w, 0, 0:HALF], lhs, keys[:, 0:HALF], True, True)
                mm(wide[buf][0:w, 1, 0:HALF], lhs, keys[:, TOK - HALF:TOK], True, True).then_inc(s_rough, 1)

            def bias_product():
                pe.wait_ge(s_b1, 3)
                pe.wait_ge(s_w2, 3)
                group = [e for e in range(E) if e not in POOLED]
                for e in group:
                    last = mm(mix[0:E, D:2 * D], b1_diag[:, e, :], w2s[:, e, :], e == group[0], e == group[-1])
                last.then_inc(s_bias, 1)

            def transpose_max(i):
                pe.wait_ge(s_max, NT * i + NT)
                for t in range(NT):
                    w, j = tile_size(t), t // 2
                    last = pe.transpose(wide[1][0:D + 1, t % 2, j * P:j * P + w], row_max[0:w, t, :], ident[0:w, 0:w])
                last.then_inc(s_maxt, 1)

            def scores(i, t):
                if t == 0:
                    pe.wait_ge(s_shift, i + 1)
                elif t >= 2:
                    pe.wait_ge(s_prob, NT * i + t - 1)
                a, w = tile_start(t), key_size(t)
                for s in range(2):
                    cols = slice(s * HALF, (s + 1) * HALF)
                    mm(wide[t % 2][0:w, s, 0:HALF], keys[:, a:a + w], q_hi[:, cols], True, False)
                    last = mm(wide[t % 2][0:w, s, 0:HALF], keys1[:, a:a + w], q_lo[:, cols], False, True)
                last.then_inc(s_score, 1)

            def weigh_values(i, t, buf):
                pe.wait_ge(s_prob, NT * i + t + 1)
                w = key_size(t)
                for u in range(NT):
                    a, n = tile_start(u), tile_size(u)
                    last = mm(small[0:n, u * (D + 1):(u + 1) * (D + 1)], probs[0:w, t, a:a + n], xn1[buf][0:w, t, D:2 * D + 1],
                              t == 0 and u == 0, t == NT - 1)
                if t == NT - 1:
                    last.then_inc(s_pv, 1)

            def gate_logits(i, par):
                pe.wait_ge(s_x2lo, i + 1)
                pe.wait_ge(s_attn, 2 * i + 2)
                pe.wait_ge(s_w1lo, 2)
                for t in range(NT):
                    a, w = tile_start(t), tile_size(t)
                    dst = small[0:w, t * E:(t + 1) * E]
                    mm(dst, x2[par][:, a:a + w], gw_hi[:], True, False)
                    last = mm(dst, x2[par][:, a:a + w], gw_lo[:], False, True)
                last.then_inc(s_lg, 1)

            def transpose_gates(i):
                pe.wait_ge(s_gates, i + 1)
                for t in range(NT):
                    w, j = tile_size(t), t // 2
                    last = pe.transpose(wide[0][0:E, t % 2, j * P:j * P + w], gates[0:w, t, :], ident[0:w, 0:w])
                last.then_inc(s_gt, 1)

            def gated_biases(n):
                pe.wait_ge(s_biasw, 1)
                pe.wait_ge(s_gtc, n + 1)
                pe.wait_ge(s_mixc, CREDIT + n)
                for s in range(2):
                    last = mm(mix[s * D:(s + 1) * D, 0:HALF], bias_w[:], gates_t[:, s * HALF:(s + 1) * HALF],
                              True, False)
                last.then_inc(s_bmm, 1)

            def first_layer(n, e, buf):
                for s in range(2):
                    if e > 0 and e - 1 in POOLED:
                        pe.wait_ge(s_relu, hidden_before(n, e - 1, s, True))
                    elif e > 0:
                        pe.wait_ge(s_hid, hidden_before(n, e - 1, s, False))
                    rhs = x2[buf][:, s * HALF:(s + 1) * HALF]
                    mm(up[s][:, 0:HALF], w1_hi[:, e, :], rhs, True, False)
                    mm(up[s][:, 0:HALF], w1_lo[:, e, :], rhs, False, True).then_inc(s_up, 1)

            def second_layer(n, e):
                if e in POOLED:
                    pe.wait_ge(s_phid, CREDIT + hidden_before(n, e, 1, True))
                else:
                    pe.wait_ge(s_hid, hidden_before(n, e, 1, False))
                for s in range(2):
                    last = mm(mix[s * D:(s + 1) * D, 0:HALF], w2s[:, e, :], hidden[:, e % 2, s, :], False, e == E - 1)
                last.then_inc(s_down, 1)

            def iteration(i, par, moe, att, conv):
                for e in range(E):
                    if moe:
                        if e == 0:
                            gated_biases(i - 1)
                        first_layer(i - 1, e, 1 - par)
                    if att and e == 11:
                        pe.wait_ge(s_ln[1], i + 1)
                        to_features(wide[1], xn2[par], s_t2)
                    if moe and e > 0:
                        second_layer(i - 1, e - 1)
                    if conv and e == 0:
                        if moe:
                            pe.wait_ge(s_ftc, CREDIT + i - 1)
                        transpose_x(i + 1, 0)
                    if att and e == 0:
                        max_scores(i, 4)
                        max_scores(i, 5)
                    if conv and e == 0:
                        transpose_x(i + 1, 1)
                    if att and e == 1:
                        transpose_max(i)
                    if att and 2 <= e < 5:
                        scores(i, 2 * (e - 2))
                        scores(i, 2 * (e - 2) + 1)
                    if conv and 1 <= e < 4:
                        convolve(i + 1, CONV_CUTS[e - 1], CONV_CUTS[e])
                    if conv and e == 4:
                        pe.wait_ge(s_convc, i + 2)
                        to_tokens(conv_t, s_ht)
                    if att and 5 <= e < 8:
                        if conv and e == 5:
                            pe.wait_ge(s_h0, i + 2)
                        weigh_values(i, 2 * (e - 5), par)
                        weigh_values(i, 2 * (e - 5) + 1, par)
                    if conv and e == 8:
                        pe.wait_ge(s_ln[0], i + 2)
                        pe.wait_ge(s_prob, NT * i + NT)
                        to_features(wide[1], xn1[1 - par], s_t1)
                    if not moe and e == 2:
                        pe.wait_ge(s_moe_in, 16 * MOE_LOADS)
                        pe.transpose(mix[:, 0:E], b1_rows[:], ident[0:E, 0:E]).then_inc(s_b1t, 1)
                    if not moe and e == 9:
                        bias_product()
                    if conv and e == 10:
                        project(i + 1)
                    if att and e == 12:
                        gate_logits(i, par)
                    if att and e == 14:
                        if conv:
                            pe.wait_ge(s_qhi, i + 2)
                            pe.wait_ge(s_qlo, i + 2)
                        transpose_gates(i)
                if moe:
                    second_layer(i - 1, E - 1)
                if conv:
                    for t in range(4):
                        max_scores(i + 1, t)
                if moe:
                    pe.wait_ge(s_mixc, CREDIT + i)
                    if att:
                        pe.wait_ge(s_logit, 2 * i + 2)
                    to_tokens(moe_t, s_ft)

            for t in range(4):
                max_scores(0, t, False)
            pipeline(pe, iteration)


INPUTS = ["x", "L0_tok_w_real", "L0_tok_w_imag", "L0_tok_phases", "L0_attn_Wq", "L0_attn_Wk", "L0_ffn_gate_w",
          "L0_ffn_gate_b", "L0_ffn_w1", "L0_ffn_b1", "L0_ffn_w2", "L0_ffn_b2", "L0_ffn_gamma", "L0_ffn_beta"]


def kernel(**inputs):
    import numpy as np
    import concourse.bacc as bacc
    from concourse.bass_utils import run_bass_kernel_spmd

    nc = bacc.Bacc("TRN2", target_bir_lowering=False, num_devices=1)
    arrays, args = {}, []
    for name in INPUTS:
        a = np.ascontiguousarray(inputs[name])
        arrays[name] = a
        args.append(nc.dram_tensor(name, a.shape, F32, kind="ExternalInput").ap())
    out = nc.dram_tensor("out", (BATCH, TOK, D), F32, kind="ExternalOutput").ap()
    build(nc, *args, out)
    r = run_bass_kernel_spmd(nc, [arrays], core_ids=[0])
    return r.results[0]["out"]
```

```python
import math
from contextlib import ExitStack

import concourse.bass as bass
from concourse import mybir

F32 = mybir.dt.float32
F32R = mybir.dt.float32r
U32 = mybir.dt.uint32
ALU = mybir.AluOpType
ACT = mybir.ActivationFunctionType
AX = mybir.AxisListType

BATCH, S_IN, D, TAPS = 8, 750, 64, 16
TOK = S_IN - TAPS + 1
HALF = (TOK + 1) // 2
TOKP = 2 * HALF
P = 128
BLOCKS = -(-HALF // P)
NT = 2 * BLOCKS
LAST = HALF - (BLOCKS - 1) * P
FULL = NT - 2
CHUNKS = TAPS // 2
XT_TILES = -(-S_IN // P)
XT_PART = XT_TILES // 2 * P
XT_LAST = S_IN - (XT_TILES - 1) * P
E, F = 16, 128
ROW_GATES = E // 4
NEAR, MIDDLE = 5, 8
SPREAD = 10
POOLED = (10, 13, 14)
HIDDEN = 4
AHEAD = 4
CONV_CUTS = (0, 3, 6, CHUNKS)
EPS = 1e-5
BANK = 512
ROUND = 1.5 * 2.0 ** 23
TWO_PI_HI = 6.28125
TWO_PI_LO = 2 * math.pi - TWO_PI_HI
PI_BELOW = 3.1415925
CONST = 13
MOE_LOADS = 10
CREDIT = 1


def tile_start(t):
    return (t % 2) * HALF + (t // 2) * P


def tile_size(t):
    return P if t < FULL else LAST


def key_size(t):
    return tile_size(t) - (1 if tile_start(t) + tile_size(t) > TOK else 0)


def row_of(rows, e):
    p = 32 * (e // ROW_GATES)
    return rows[p:p + 1, e % ROW_GATES, :]


def hidden_before(n, e, s, pooled):
    group = [k for k in range(E) if (k in POOLED) == pooled]
    return 2 * len(group) * n + 2 * sum(k < e for k in group) + (s + 1 if e in group else 0)


def seconds_at(slot):
    return [e for e in range(E) if max(k + (2 if k in POOLED else 1) for k in range(e + 1)) == slot
            or (slot == E and max(k + (2 if k in POOLED else 1) for k in range(e + 1)) > E)]


def along(ap, shape):
    return ap.unsqueeze(2).broadcast_to(shape)


def build(nc, x, w_real, w_imag, phases, wq, wk, gate_w, gate_b, w1, b1, w2, b2, gamma, beta, out):
    ctx = ExitStack()
    with ctx:
        def sb(name, shape, dt=F32):
            return ctx.enter_context(nc.sbuf_tensor(name, shape, dt))

        def ps(name, shape):
            return ctx.enter_context(nc.psum_tensor(name, shape, F32))

        def sem(name):
            return ctx.enter_context(nc.semaphore(name))

        ident = sb("ident", [P, P])
        iota = sb("iota", [P, E])
        phase = sb("phase", [D, TAPS])
        trig = sb("trig", [D, 6, TAPS])
        conv_w = sb("conv_w", [P, CHUNKS, D])
        wq2 = sb("wq2", [D, 2, D])
        wk2 = sb("wk2", [D, 2, D])
        a_hi = sb("a_hi", [P, P], F32R)
        a_lo = sb("a_lo", [P, P], F32R)
        w1_raw = sb("w1_raw", [P, E, F])
        w1_hi = sb("w1_hi", [P, E, F], F32R)
        w1_lo = sb("w1_lo", [P, E, F], F32R)
        w2_sum = sb("w2_sum", [P, E])
        w2s = sb("w2s", [P, E, D])
        b1_rows = sb("b1_rows", [E, F])
        b1_neg = sb("b1_neg", [P, E])
        b1_pos = sb("b1_pos", [P, E])
        b1_diag = sb("b1_diag", [P, E, E])
        b2_raw = sb("b2_raw", [E, D])
        b2_sum = sb("b2_sum", [E, 1])
        b2s = sb("b2s", [E, D])
        bias_w = sb("bias_w", [E, D])
        gw_raw = sb("gw_raw", [P, E])
        gw = sb("gw", [P, 2, E], F32R)
        gb = sb("gb", [P, E])
        gam = sb("gam", [P, D])
        bet = sb("bet", [P, D])
        power = sb("power", [P, NT])

        xx = sb("xx", [P, XT_TILES, 2 * D])
        xt = sb("xt", [P, S_IN])
        conv_t = sb("conv_t", [P, HALF])
        h0 = [sb(f"h0_{k}", [P, NT, D]) for k in range(2)]
        xn1 = [sb(f"xn1_{k}", [P, NT, 2 * D]) for k in range(2)]
        keys = sb("keys", [P, TOKP], F32R)
        keys1 = sb("keys1", [D + 1, TOKP], F32R)
        q_hi = sb("q_hi", [P, TOKP], F32R)
        q_lo = sb("q_lo", [D + 1, TOKP], F32R)
        row_max = sb("row_max", [P, NT, D + 1])
        probs = sb("probs", [P, NT, TOKP])
        prob_sum = sb("prob_sum", [P, TOKP])
        ones = sb("ones", [P, 1])
        rden = sb("rden", [P, NT])
        attn_t = sb("attn_t", [P, HALF])
        attn = sb("attn", [P, NT, D])
        h1 = [sb(f"h1_{k}", [P, NT, D]) for k in range(2)]
        xn2 = [sb(f"xn2_{k}", [P, NT, 2 * D]) for k in range(2)]
        x2 = [sb(f"x2_{k}", [P, TOKP], F32R) for k in range(2)]
        biased = sb("biased", [P, NT, E])
        logits = sb("logits", [P, NT, E])
        top = sb("top", [P, NT, 8])
        top_at = sb("top_at", [P, NT, 8], U32)
        at = sb("at", [P, NT, 2])
        gap = sb("gap", [P, NT])
        expgap = sb("expgap", [P, NT])
        wsum = sb("wsum", [P, NT])
        wtop = sb("wtop", [P, 2, NT])
        pick = sb("pick", [P, 2, NT, E])
        gates = sb("gates", [P, NT, E])
        gates_t = sb("gates_t", [E, TOKP])
        gates_row = sb("gates_row", [P, ROW_GATES, TOKP])
        gates_all = sb("gates_all", [P, E, TOKP])
        raw = gates_all[:].rearrange("p e n -> p (e n)")
        wr, wi = (raw[0:D, k * D * TAPS:(k + 1) * D * TAPS] for k in range(2))
        w_sin, w_eff = (raw[0:D, k * D * TAPS:(k + 1) * D * TAPS].rearrange("p (k i) -> p k i", i=D)
                        for k in (2, 3))
        relu = sb("relu", [P, 2, 2, HALF])
        hidden = sb("hidden", [P, HIDDEN, 2, HALF])
        moe_t = sb("moe_t", [P, HALF])
        moe_tok = sb("moe_tok", [P, NT, D])
        res = [sb(f"res{k}", [P, NT, D]) for k in range(3)]
        outs = sb("outs", [P, NT, D])
        mean_sum = sb("mean_sum", [P, NT])
        cen0 = [sb(f"cen0_{k}", [P, NT, D]) for k in range(2)]
        cen1 = sb("cen1", [P, NT, D])
        cen2 = sb("cen2", [P, NT, D])
        cen_sq = [sb(f"cen_sq{k}", [P, NT, D]) for k in range(3)]
        var = [sb(f"var{k}", [P, NT]) for k in range(3)]
        var_eps = [sb(f"var_eps{k}", [P, NT]) for k in range(3)]
        rstd = [sb(f"rstd{k}", [P, NT]) for k in range(3)]

        wide = [ps(f"wide{k}", [P, 2, BANK]) for k in range(2)]
        small = ps("small", [P, BANK])
        up = [ps(f"up{k}", [P, BANK]) for k in range(2)]
        mix = ps("mix", [P, BANK])

        s_phase = sem("phases_loaded")
        s_conv_in = sem("conv_w_loaded")
        s_wqk_in = sem("wqk_loaded")
        s_moe_in = sem("moe_w_loaded")
        s_const = sem("constants_made")
        s_zero = sem("zeros_made")
        s_trig = sem("trig_steps")
        s_sin = sem("sin_done")
        s_weff = sem("w_eff_steps")
        s_wt = sem("conv_w_transposed")
        s_wc = sem("conv_w_ready")
        s_a = sem("a_product")
        s_ahi = sem("a_hi_ready")
        s_alo = sem("a_lo_ready")
        s_w1hi = sem("w1_hi_ready")
        s_w1lo = sem("w1_lo_ready")
        s_b1t = sem("b1_transposed")
        s_b1 = sem("b1_ready")
        s_w2 = sem("w2_steps")
        s_bias = sem("bias_product")
        s_biasw = sem("bias_w_ready")
        s_x = sem("x_loaded")
        s_xt = sem("x_transposed")
        s_xtc = sem("xt_copied")
        s_conv = sem("conv_done")
        s_convc = sem("conv_copied")
        s_ht = sem("h_transposed")
        s_h0 = sem("h0_copied")
        s_mean = sem("mean_summed")
        s_cen = [sem(f"ln{k}_centred") for k in range(3)]
        s_var = [sem(f"ln{k}_variance") for k in range(3)]
        s_eps = [sem(f"ln{k}_eps_added") for k in range(3)]
        s_rstd = [sem(f"ln{k}_rstd") for k in range(3)]
        s_ln = [sem(f"ln{k}_normed") for k in range(2)]
        s_t1 = sem("xn1_transposed")
        s_khi = sem("keys_hi_ready")
        s_kone = sem("keys1_ready")
        s_klo = sem("keys_lo_ready")
        s_q = sem("q_product")
        s_qhi = sem("q_hi_ready")
        s_qlo = sem("q_lo_ready")
        s_rough = sem("max_scores_ready")
        s_max = sem("max_reduced")
        s_maxt = sem("max_transposed")
        s_shift = sem("shift_ready")
        s_score = sem("scores_ready")
        s_prob = sem("probs_ready")
        s_pv = sem("attention_summed")
        s_psum = sem("probabilities_added")
        s_den = sem("denominator_ready")
        s_rden = sem("denominator_inverted")
        s_pvc = sem("attention_sum_copied")
        s_at = sem("attention_transposed")
        s_attn = sem("attention_scaled")
        s_h1 = sem("h1_ready")
        s_t2 = sem("xn2_transposed")
        s_x2hi = sem("x2_hi_ready")
        s_x2lo = sem("x2_lo_ready")
        s_lg = sem("logits_product")
        s_biased = sem("bias_in_logits")
        s_logit = sem("logits_ready")
        s_top = sem("top_values")
        s_topi = sem("top_indices")
        s_gap = sem("gap_ready")
        s_egap = sem("exp_gap_ready")
        s_gate = sem("gate_steps")
        s_gates = sem("gates_ready")
        s_gt = sem("gates_transposed")
        s_gtc = sem("gates_copied")
        s_flat = sem("gates_flattened")
        s_dpace = sem("max_paced")
        s_pace = sem("broadcast_paced")
        s_gall = sem("gates_broadcast")
        s_bmm = sem("bias_added")
        s_up = sem("up_ready")
        s_hid = sem("hidden_ready")
        s_relu = sem("relu_done")
        s_phid = sem("pooled_hidden_ready")
        s_down = sem("down_done")
        s_mixc = sem("mix_copied")
        s_ft = sem("mix_transposed")
        s_ftc = sem("mix_tokens_copied")
        s_fin = sem("final_steps")
        s_tail = sem("last_steps")
        s_res = sem("result_ready")
        s_out = sem("stored")

        block = ctx.enter_context(nc.Block())

        def pipeline(eng, opening, iteration):
            opening()
            iteration(1, 1, True, True, True, True)
            pairs = (BATCH - 3) // 2
            with eng.Fori(0, pairs) as k:
                iteration(2 * k + 2, 0, False, True, True, True)
                iteration(2 * k + 3, 1, False, True, True, True)
            for i in range(2 + 2 * pairs, BATCH + 1):
                iteration(i, i % 2, False, i < BATCH, i < BATCH - 1, i < BATCH - 2)

        def split(ap):
            return ap.rearrange("p (s n) -> p s n", s=2)

        def gate_hidden(eng, n, e):
            for s in range(2):
                eng.wait_ge(s_relu, hidden_before(n, e, s, True))
                if s == 0:
                    eng.wait_ge(s_down, HIDDEN + E * n + e - HIDDEN + 1)
                eng.tensor_tensor(hidden[:, e % HIDDEN, s, :], relu[:, POOLED.index(e) % 2, s, :],
                                   gates_all[:, e, s * HALF:(s + 1) * HALF], ALU.mult).then_inc(s_phid, 1)

        @block.sync
        def _(sp):
            def load_x(b):
                rows = (XT_TILES - 1) * P
                flat = x[b].rearrange("t c -> (t c)")
                for h in range(2):
                    sp.dma_start(xx[:, 0:XT_TILES - 1, h * D:(h + 1) * D],
                                 flat[h * D:h * D + rows * D].rearrange("(i p c) -> p i c", p=P, c=D)
                                 ).then_inc(s_x, 16)
                    n = XT_LAST - h
                    sp.dma_start(xx[0:n, XT_TILES - 1, h * D:(h + 1) * D],
                                 flat[(rows + h) * D:(rows + h + n) * D].rearrange("(p c) -> p c", c=D)
                                 ).then_inc(s_x, 16)

            sp.sem_inc(s_out, 16 * CREDIT)
            sp.dma_start(phase[:], phases.partition_broadcast(D)).then_inc(s_phase, 16)
            sp.dma_start(wr, w_real.rearrange("o i k -> o (i k)")).then_inc(s_conv_in, 16)
            sp.dma_start(wi, w_imag.rearrange("o i k -> o (i k)")).then_inc(s_conv_in, 16)
            sp.wait_ge(s_zero, 1)
            load_x(0)
            for h in range(2):
                sp.dma_start(wq2[:, h, :], wq).then_inc(s_wqk_in, 16)
                sp.dma_start(wk2[:, h, :], wk).then_inc(s_wqk_in, 16)
            for h in range(2):
                sp.dma_start(gw_raw[h * D:(h + 1) * D, :], gate_w).then_inc(s_moe_in, 16)
                sp.dma_start(w1_raw[h * D:(h + 1) * D, :, :], w1.rearrange("e h f -> h e f")).then_inc(s_moe_in, 16)
            sp.dma_start(w2s[:], w2.rearrange("e f h -> f e h")).then_inc(s_moe_in, 16)
            sp.dma_start(b1_rows[:], b1).then_inc(s_moe_in, 16)
            sp.dma_start(b2_raw[:], b2).then_inc(s_moe_in, 16)
            sp.dma_start(gb[:], gate_b.partition_broadcast(P)).then_inc(s_moe_in, 16)
            sp.dma_start(gam[:], gamma.partition_broadcast(P)).then_inc(s_moe_in, 16)
            sp.dma_start(bet[:], beta.partition_broadcast(P)).then_inc(s_moe_in, 16)

            def store(b):
                sp.wait_ge(s_conv_in, 32)
                sp.wait_ge(s_res, CREDIT + b + 1)
                for h in range(2):
                    sp.dma_start(out[b, h * HALF:h * HALF + (BLOCKS - 1) * P, :].rearrange("(j p) c -> p j c", p=P),
                                 outs[:, h:FULL:2, :]).then_inc(s_out, 16)
                for t in range(FULL, NT):
                    sp.dma_start(out[b, tile_start(t):tile_start(t) + key_size(t), :],
                                 outs[0:key_size(t), t, :]).then_inc(s_out, 16)

            def load_next(n):
                sp.wait_ge(s_conv_in, 32)
                sp.wait_ge(s_xt, 2 * n)
                load_x(n)

            for n in range(1, AHEAD):
                load_next(n)
            with sp.Fori(0, BATCH - AHEAD) as b:
                load_next(b + AHEAD)
                store(b)
            for b in range(BATCH - AHEAD, BATCH):
                store(b)
            sp.wait_ge(s_out, 16 * CREDIT + 64 * BATCH)

        @block.gpsimd
        def _(pool):
            pool.sem_inc(s_res, CREDIT)
            pool.sem_inc(s_cen[2], CREDIT)
            pool.sem_inc(s_phid, CREDIT)
            pool.memset(xx[:, XT_TILES - 1, :], 0.0).then_inc(s_zero, 1)
            pool.memset(ident[:], 0.0).then_inc(s_zero, 1)
            pool.iota(iota[:], [[1, E]], base=0, channel_multiplier=0,
                      allow_small_or_imprecise_dtypes=True).then_inc(s_const, 1)
            pool.wait_ge(s_zero, 2)
            pool.affine_select(out=ident[:], in_=ident[:], compare_op=ALU.not_equal, fill=1.0,
                               base=0, pattern=[[-1, P]], channel_multiplier=1).then_inc(s_const, 1)
            pool.memset(power[:], -0.5).then_inc(s_const, 1)
            for t in (*h0, row_max, attn, cen1, logits, moe_tok):
                pool.memset(t[:], 0.0).then_inc(s_const, 1)
            pool.memset(ones[:], 1.0).then_inc(s_const, 1)
            pool.memset(b1_diag[:], 0.0).then_inc(s_const, 1)
            pool.wait_ge(s_const, CONST - 1)
            pool.memset(keys1[D:D + 1, :].bitcast(F32), 1.0).then_inc(s_const, 1)
            pool.wait_ge(s_const, CONST)

            def deviation(k, n):
                pool.wait_ge(s_var[k], n + 1)
                pool.sem_inc(s_pace, 1)
                pool.tensor_scalar(var_eps[k][:], var[k][:], EPS, None, ALU.add).then_inc(s_eps[k], 1)
                pool.wait_ge(s_eps[k], n + 1)
                pool.tensor_tensor(rstd[k][:], var_eps[k][:], power[:], ALU.pow).then_inc(s_rstd[k], 1)

            def broadcast(n, e, again):
                if again:
                    pool.wait_ge(s_hid, hidden_before(n - 1, e, 1, False))
                if e > 0:
                    pool.wait_ge(s_gall, E * n + e)
                if again or e > 0:
                    pool.sem_inc(s_pace, 1)
                pool.partition_broadcast(gates_all[:, e, :], row_of(gates_row, e), P).then_inc(s_gall, 1)

            def gamma_beta(m, buf):
                pool.wait_ge(s_rstd[2], m + 1)
                pool.tensor_tensor(res[0][:], cen2[:], along(rstd[2][:], [P, NT, D]), ALU.mult).then_inc(s_fin, 1)
                pool.wait_ge(s_fin, 3 * m + 1)
                pool.tensor_tensor(res[1][:], res[0][:], gam[:].unsqueeze(1).broadcast_to([P, NT, D]), ALU.mult).then_inc(s_fin, 1)
                pool.wait_ge(s_fin, 3 * m + 2)
                pool.tensor_tensor(res[2][:], res[1][:], bet[:].unsqueeze(1).broadcast_to([P, NT, D]), ALU.add).then_inc(s_fin, 1)
                pool.wait_ge(s_fin, 3 * m + 3)
                pool.wait_ge(s_out, 16 * CREDIT + 64 * m)
                pool.tensor_tensor(outs[:], res[2][:], h1[buf][:], ALU.add).then_inc(s_res, 1)

            def iteration(i, par, first, att, conv, ahead):
                for e in range(SPREAD, E):
                    broadcast(i - 1, e, False)
                pool.wait_ge(s_gall, E * i)
                if not att:
                    deviation(2, BATCH - 2)
                    gamma_beta(BATCH - 2, par)
                    pool.wait_ge(s_res, CREDIT + BATCH - 1)
                    pool.tensor_tensor(res[2][:], h1[1 - par][:], bet[:].unsqueeze(1).broadcast_to([P, NT, D]),
                                       ALU.add).then_inc(s_fin, 1)
                    deviation(2, BATCH - 1)
                    return
                deviation(1, i)
                gate_hidden(pool, i - 1, POOLED[0])
                pool.wait_ge(s_attn, 2 * i + 2)
                pool.tensor_tensor(h1[par][:], attn[:], h0[par][:], ALU.add).then_inc(s_h1, 1)
                for e in POOLED[1:]:
                    gate_hidden(pool, i - 1, e)
                pool.wait_ge(s_phid, CREDIT + hidden_before(i, 0, -1, True))
                pool.wait_ge(s_h1, i + 1)
                pool.wait_ge(s_flat, 16 * (i + 1))
                pool.sem_inc(s_pace, 1)
                for e in range(2):
                    broadcast(i, e, True)
                pool.wait_ge(s_gall, E * i + 2)
                m = i - 1
                pool.wait_ge(s_hid, hidden_before(i, 0, -1, False))
                pool.wait_ge(s_ftc, CREDIT + m + 1)
                pool.tensor_tensor(cen2[:], moe_tok[:], xn2[1 - par][:, :, 0:D], ALU.add).then_inc(s_cen[2], 1)
                pool.wait_ge(s_cen[2], CREDIT + i)
                for e in range(2, NEAR):
                    broadcast(i, e, False)
                if ahead:
                    pool.wait_ge(s_gall, E * i + NEAR)
                    deviation(0, i + 2)
                    pool.wait_ge(s_rstd[0], i + 3)
                for e in range(NEAR, MIDDLE):
                    broadcast(i, e, False)
                if conv:
                    pool.wait_ge(s_gall, E * i + MIDDLE)
                    deviation(2, m)
                    gamma_beta(m, 1 - par)
                    pool.wait_ge(s_res, CREDIT + i)
                for e in range(MIDDLE, SPREAD):
                    broadcast(i, e, False)
                pool.wait_ge(s_gall, E * i + SPREAD)

            def opening():
                deviation(0, 1)
                deviation(1, 0)
                pool.wait_ge(s_attn, 2)
                pool.tensor_tensor(h1[0][:], attn[:], h0[0][:], ALU.add).then_inc(s_h1, 1)
                pool.wait_ge(s_rstd[1], 1)
                pool.wait_ge(s_h1, 1)
                pool.wait_ge(s_flat, 16)
                for e in range(NEAR):
                    broadcast(0, e, False)
                pool.wait_ge(s_gall, NEAR)
                deviation(0, 2)
                pool.wait_ge(s_rstd[0], 3)
                for e in range(NEAR, SPREAD):
                    broadcast(0, e, False)
                pool.wait_ge(s_gall, SPREAD)

            deviation(0, 0)
            pipeline(pool, opening, iteration)

        @block.scalar
        def _(act):
            def copy(dst, src, scale=1.0):
                return act.activation(dst, src, ACT.Copy, scale=scale)

            act.sem_inc(s_mixc, CREDIT)
            act.sem_inc(s_ftc, CREDIT)
            act.wait_ge(s_trig, 6)
            act.activation(trig[:, 5, :], trig[:, 3, :], ACT.Sin).then_inc(s_sin, 1)
            act.wait_ge(s_trig, 8)
            act.activation(trig[:, 4, :], trig[:, 1, :], ACT.Sin).then_inc(s_sin, 1)
            def xt_copy(n, part, src):
                act.wait_ge(s_xt, 2 * n + part + 1)
                if part == 0:
                    act.wait_ge(s_conv, n)
                lo = part * XT_PART
                w = min(XT_PART, S_IN - lo)
                copy(xt[:, lo:lo + w], src[:, 0:w]).then_inc(s_xtc, 1)

            def conv_copy(n, src=small):
                act.wait_ge(s_conv, n + 1)
                act.wait_ge(s_ht, n)
                copy(conv_t[:], src[:, 0:HALF]).then_inc(s_convc, 1)

            def tokens_copy(dst, done, src=small):
                src = src[:, 0:NT * D].rearrange("p (t c) -> p t c", c=D)
                copy(dst[:, 0:FULL, :], src[:, 0:FULL, :])
                copy(dst[0:LAST, FULL:NT, :], src[0:LAST, FULL:NT, :]).then_inc(done, 1)

            def h0_copy(n, buf, src=small):
                act.wait_ge(s_ht, n + 1)
                tokens_copy(h0[buf], s_h0, src)

            def variance(k, src, n):
                act.wait_ge(s_cen[k], n + 1 + (CREDIT if k == 2 else 0))
                for t in range(NT):
                    last = act.activation(cen_sq[k][:, t, :], src[:, t, :], ACT.Square, scale=D ** -0.5,
                                          accum_out=var[k][:, t:t + 1])
                last.then_inc(s_var[k], 1)

            def keys_hi(n):
                act.wait_ge(s_t1, n + 1)
                act.wait_ge(s_prob, NT * n)
                copy(split(keys[:]), wide[1][:, :, 0:HALF]).then_inc(s_khi, 1)

            def keys_hi_again(n):
                copy(split(keys1[0:D, :]), wide[1][0:D, :, 0:HALF]).then_inc(s_kone, 1)

            def query_hi(n):
                act.wait_ge(s_q, n + 1)
                copy(split(q_hi[:]), wide[0][:, :, 0:HALF]).then_inc(s_qhi, 1)

            xt_copy(0, 0, up[0])
            xt_copy(0, 1, up[1])
            act.wait_ge(s_wt, 1)
            copy(conv_w[:].rearrange("p k o -> p (k o)"), small[:]).then_inc(s_wc, 1)
            act.wait_ge(s_a, 1)
            copy(a_hi[:], wide[0][:, 0, 0:P], D ** -0.5).then_inc(s_ahi, 1)
            conv_copy(0)
            h0_copy(0, 0)
            variance(0, cen0[0], 0)
            keys_hi(0)
            keys_hi_again(0)
            query_hi(0)
            act.wait_ge(s_moe_in, 16 * MOE_LOADS)
            copy(gw[:, 0, :], gw_raw[:]).then_inc(s_w1hi, 1)
            copy(w1_hi[:], w1_raw[:]).then_inc(s_w1hi, 1)

            def rectify(n, e):
                k = POOLED.index(e)
                for s in range(2):
                    act.wait_ge(s_up, 2 * E * n + 2 * e + s + 1)
                    if s == 0:
                        used = hidden_before(n, POOLED[k - 2], 1, True) if k >= 2 else hidden_before(n, e, -1, True)
                        act.wait_ge(s_phid, CREDIT + used)
                    act.activation(relu[:, k % 2, s, :], up[s][:, 0:HALF], ACT.Relu, bias=b1_pos[:, e:e + 1]).then_inc(s_relu, 1)

            def exponentials(i, first, end):
                for t in range(first, end):
                    act.wait_ge(s_score, NT * i + t + 1)
                    if t == 0:
                        act.wait_ge(s_pv, i)
                    w = key_size(t)
                    act.activation(split(probs[0:w, t, :]), wide[t % 2][0:w, :, 0:HALF], ACT.Exp).then_inc(s_prob, 1)

            def shift(i):
                act.wait_ge(s_maxt, i + 1)
                copy(split(q_lo[D:D + 1, :]), wide[1][D:D + 1, :, 0:HALF], -1.0).then_inc(s_shift, 1)

            def attention_copy(i):
                act.wait_ge(s_pv, i + 1)
                copy(attn_t[:], small[:, 0:HALF]).then_inc(s_pvc, 1)

            def x2_hi(i, buf):
                act.wait_ge(s_t2, i + 1)
                copy(split(x2[buf][:]), wide[1][:, :, 0:HALF]).then_inc(s_x2hi, 1)

            def exp_gap(i):
                act.wait_ge(s_gap, i + 1)
                act.activation(expgap[:], gap[:], ACT.Exp).then_inc(s_egap, 1)

            def gates_to_rows(i, again):
                act.wait_ge(s_gt, i + 1)
                if again:
                    act.wait_ge(s_bmm, i)
                    act.wait_ge(s_flat, 16 * i)
                copy(split(gates_t[:]), wide[0][0:E, :, 0:HALF]).then_inc(s_gtc, 1)
                act.wait_ge(s_gtc, i + 1)
                if again:
                    act.wait_ge(s_gall, E * i)
                act.dma_start(gates_row[0:P:32, :, :], gates_t[:]).then_inc(s_flat, 16)

            def opening():
                xt_copy(1, 0, up[0])
                xt_copy(1, 1, up[1])
                shift(0)
                exponentials(0, 0, 4)
                conv_copy(1, up[0])
                exponentials(0, 4, NT)
                h0_copy(1, 1, up[1])
                variance(0, cen0[1], 1)
                attention_copy(0)
                xt_copy(2, 0, up[0])
                xt_copy(2, 1, up[1])
                variance(1, cen1, 0)
                keys_hi(1)
                keys_hi_again(1)
                query_hi(1)
                x2_hi(0, 0)
                exp_gap(0)
                gates_to_rows(0, False)
                conv_copy(2, up[0])
                act.wait_ge(s_h1, 1)
                h0_copy(2, 0, up[1])

            def iteration(i, par, first, att, conv, ahead):
                if not first:
                    variance(2, cen2, i - 2)
                if att:
                    shift(i)
                    exponentials(i, 0, 2)
                if conv:
                    variance(0, cen0[1 - par], i + 1)
                if att:
                    exponentials(i, 2, NT)
                if conv:
                    keys_hi(i + 1)
                    keys_hi_again(i + 1)
                    query_hi(i + 1)
                if att:
                    attention_copy(i)
                if ahead:
                    xt_copy(i + 2, 0, wide[0][:, 0, :])
                    xt_copy(i + 2, 1, wide[0][:, 1, :])
                if att:
                    variance(1, cen1, i)
                rectify(i - 1, POOLED[0])
                if att:
                    x2_hi(i, par)
                if ahead:
                    conv_copy(i + 2)
                rectify(i - 1, POOLED[1])
                if att:
                    exp_gap(i)
                rectify(i - 1, POOLED[2])
                if ahead:
                    act.wait_ge(s_h1, i + 1)
                    h0_copy(i + 2, par)
                if att:
                    gates_to_rows(i, True)
                act.wait_ge(s_down, HIDDEN + E * i)
                act.wait_ge(s_ft, CREDIT + i - 1)
                copy(moe_t[:], mix[:, 0:HALF]).then_inc(s_mixc, 1)
                if att:
                    act.wait_ge(s_ft, CREDIT + i)
                    act.wait_ge(s_cen[2], CREDIT + i - 1)
                    tokens_copy(moe_tok, s_ftc)

            pipeline(act, opening, iteration)
            variance(2, cen2, BATCH - 1)

        @block.vector
        def _(dve):
            dve.wait_ge(s_phase, 16)
            ph, turns, r, c = phase[:], trig[:, 0, :], trig[:, 1, :], trig[:, 3, :]

            def step(n, ins):
                ins.then_inc(s_trig, 1)
                dve.wait_ge(s_trig, n)

            step(1, dve.tensor_scalar(turns, ph, 1 / (2 * math.pi), ROUND, ALU.mult, ALU.add))
            step(2, dve.tensor_scalar(trig[:, 2, :], turns, -ROUND, None, ALU.add))
            step(3, dve.scalar_tensor_tensor(r, trig[:, 2, :], -TWO_PI_HI, ph, ALU.mult, ALU.add))
            step(4, dve.scalar_tensor_tensor(turns, trig[:, 2, :], -TWO_PI_LO, r, ALU.mult, ALU.add))
            step(5, dve.scalar_tensor_tensor(trig[:, 2, :], turns, -1.0, turns, ALU.mult, ALU.max))
            step(6, dve.tensor_scalar(c, trig[:, 2, :], -1.0, math.pi / 2, ALU.mult, ALU.add))
            step(7, dve.tensor_scalar(r, turns, PI_BELOW, -PI_BELOW, ALU.min, ALU.max))
            dve.tensor_scalar(trig[:, 0, :], c, 1.0, None, ALU.mult).then_inc(s_trig, 1)
            dve.wait_ge(s_sin, 2)
            dve.wait_ge(s_conv_in, 32)
            dve.tensor_tensor(w_eff, wr.rearrange("o (i k) -> o k i", k=TAPS),
                              along(trig[:, 5, :], [D, TAPS, D]), ALU.mult).then_inc(s_weff, 1)
            dve.tensor_tensor(w_sin, wi.rearrange("o (i k) -> o k i", k=TAPS),
                              along(trig[:, 4, :], [D, TAPS, D]), ALU.mult).then_inc(s_weff, 1)
            dve.wait_ge(s_weff, 2)
            dve.tensor_tensor(w_eff, w_eff, w_sin, ALU.subtract).then_inc(s_weff, 1)
            dve.wait_ge(s_const, CONST)

            def low(dst, whole, high, scale=None):
                if scale is None:
                    return dve.tensor_tensor(dst, whole, high.bitcast(F32), ALU.subtract)
                return dve.scalar_tensor_tensor(dst, whole, scale, high.bitcast(F32), ALU.mult, ALU.subtract)

            def centre(n, buf):
                dve.wait_ge(s_h0, n + 1)
                dve.tensor_reduce(mean_sum[:], h0[buf][:], AX.X, ALU.add).then_inc(s_mean, 1)
                dve.wait_ge(s_mean, n + 1)
                dve.scalar_tensor_tensor(cen0[buf][:], along(mean_sum[:], [P, NT, D]), -1.0 / D, h0[buf][:],
                                         ALU.mult, ALU.add).then_inc(s_cen[0], 1)

            def normalise(k, dst, src, n):
                dve.wait_ge(s_rstd[k], n + 1)
                dve.tensor_tensor(dst[:, :, 0:2 * D].rearrange("p t (a c) -> p t a c", a=2),
                                  src[:].unsqueeze(2).broadcast_to([P, NT, 2, D]),
                                  rstd[k][:].unsqueeze(2).unsqueeze(3).broadcast_to([P, NT, 2, D]),
                                  ALU.mult).then_inc(s_ln[k], 1)

            def keys_lo(n):
                dve.wait_ge(s_khi, n + 1)
                low(split(keys[D:P, :]), wide[1][D:P, :, 0:HALF], split(keys[D:P, :])).then_inc(s_klo, 1)

            def query_lo(n):
                dve.wait_ge(s_qhi, n + 1)
                low(split(q_lo[0:D, :]), wide[0][0:D, :, 0:HALF], split(q_hi[0:D, :])).then_inc(s_qlo, 1)

            dve.wait_ge(s_ahi, 1)
            low(a_lo[:], wide[0][:, 0, 0:P], a_hi[:], D ** -0.5).then_inc(s_alo, 1)
            centre(0, 0)
            normalise(0, xn1[0], cen0[0], 0)
            keys_lo(0)
            query_lo(0)
            def mixture_weights():
                dve.wait_ge(s_w1hi, 2)
                low(gw[:, 1, :], gw_raw[:], gw[:, 0, :]).then_inc(s_w1lo, 1)
                low(w1_lo[:], w1_raw[:], w1_hi[:]).then_inc(s_w1lo, 1)
                dve.tensor_reduce(w2_sum[:], w2s[:], AX.X, ALU.add).then_inc(s_w2, 1)
                dve.tensor_reduce(b2_sum[:], b2_raw[:], AX.X, ALU.add).then_inc(s_w2, 1)
                dve.wait_ge(s_w2, 2)
                dve.scalar_tensor_tensor(w2s[:], along(w2_sum[:], [P, E, D]), -1.0 / D, w2s[:],
                                         ALU.mult, ALU.add).then_inc(s_w2, 1)
                dve.scalar_tensor_tensor(b2s[:], b2_sum[:].broadcast_to([E, D]), -1.0 / D, b2_raw[:],
                                         ALU.mult, ALU.add).then_inc(s_w2, 1)
                dve.wait_ge(s_b1t, 1)
                dve.tensor_scalar(b1_neg[:], mix[:, 0:E], -1.0, None, ALU.mult).then_inc(s_b1, 1)
                dve.tensor_copy(b1_pos[:], mix[:, 0:E]).then_inc(s_b1, 1)
                dve.tensor_copy(b1_diag[:].rearrange("p a b -> p (a b)")[:, 0:E * E:E + 1], mix[:, 0:E]).then_inc(s_b1, 1)
                dve.wait_ge(s_w2, 4)

            def bias_weights():
                dve.wait_ge(s_bias, 1)
                dve.tensor_tensor(bias_w[:], mix[0:E, D:2 * D], b2s[:], ALU.add).then_inc(s_biasw, 1)

            def x2_lo(i, buf):
                dve.wait_ge(s_x2hi, i + 1)
                low(split(x2[buf][D:P, :]), wide[1][D:P, :, 0:HALF], split(x2[buf][D:P, :])).then_inc(s_x2lo, 1)

            def reduce_max(i, t):
                w = tile_size(t)
                dve.wait_ge(s_rough, NT * i + t + 1)
                dve.tensor_reduce(row_max[0:w, t, D:D + 1], wide[1 - t % 2][0:w, :, 0:HALF], AX.XY,
                                  ALU.max).then_inc(s_max, 1)

            def add_probabilities(i, t):
                w = key_size(t)
                dve.wait_ge(s_prob, NT * i + t + 1)
                if t == 1:
                    dve.tensor_tensor(prob_sum[:], probs[:, 0, :], probs[:, 1, :], ALU.add).then_inc(s_psum, 1)
                else:
                    dve.wait_ge(s_psum, (NT - 1) * i + t - 1)
                    dve.tensor_tensor(prob_sum[0:w, :], prob_sum[0:w, :], probs[0:w, t, :],
                                      ALU.add).then_inc(s_psum, 1)

            def invert_denominators(i):
                den = wide[1][:, 0, 0:NT]
                dve.wait_ge(s_den, i + 1)
                dve.reciprocal(rden[:, 0:FULL], den[:, 0:FULL]).then_inc(s_rden, 1)
                dve.reciprocal(rden[0:LAST, FULL:NT], den[0:LAST, FULL:NT]).then_inc(s_rden, 1)

            def scale_attention(i):
                o = small[:, 0:NT * D].rearrange("p (t c) -> p t c", c=D)
                dve.wait_ge(s_rden, 2 * i + 2)
                dve.wait_ge(s_at, i + 1)
                dve.tensor_tensor(attn[:, 0:FULL, :], o[:, 0:FULL, :],
                                  along(rden[:, 0:FULL], [P, FULL, D]), ALU.mult).then_inc(s_attn, 1)
                dve.tensor_tensor(attn[0:LAST, FULL:NT, :], o[0:LAST, FULL:NT, :],
                                  along(rden[0:LAST, FULL:NT], [LAST, 2, D]), ALU.mult).then_inc(s_attn, 1)

            def centre_sum(i, buf):
                dve.wait_ge(s_attn, 2 * i + 2)
                dve.tensor_tensor(cen1[:], attn[:], cen0[buf][:], ALU.add).then_inc(s_cen[1], 1)

            def top_two(i):
                dve.wait_ge(s_lg, i + 1)
                lg = wide[1][:, 0, 0:2 * NT * E].rearrange("p (t a e) -> p t a e", a=2, e=E)
                dve.tensor_tensor(biased[:, 0:FULL, :], lg[:, 0:FULL, 0, :],
                                  gb[:].unsqueeze(1).broadcast_to([P, FULL, E]), ALU.add).then_inc(s_biased, 1)
                dve.tensor_tensor(biased[0:LAST, FULL:NT, :], lg[0:LAST, FULL:NT, 0, :],
                                  gb[0:LAST, :].unsqueeze(1).broadcast_to([LAST, 2, E]), ALU.add).then_inc(s_biased, 1)
                dve.wait_ge(s_biased, 2 * i + 2)
                dve.tensor_tensor(logits[:, 0:FULL, :], lg[:, 0:FULL, 1, :], biased[:, 0:FULL, :],
                                  ALU.add).then_inc(s_logit, 1)
                dve.tensor_tensor(logits[0:LAST, FULL:NT, :], lg[0:LAST, FULL:NT, 1, :], biased[0:LAST, FULL:NT, :],
                                  ALU.add).then_inc(s_logit, 1)
                dve.wait_ge(s_logit, 2 * i + 2)
                dve.sem_inc(s_dpace, 1)
                for t in range(NT):
                    dve.max(top[:, t, :], logits[:, t, :]).then_inc(s_top, 1)
                dve.wait_ge(s_top, NT * i + NT)
                dve.tensor_tensor(gap[:].unsqueeze(2), top[:, :, 1:2], top[:, :, 0:1], ALU.subtract).then_inc(s_gap, 1)

            def top_places(i):
                for t in range(NT):
                    dve.max_index(top_at[:, t, :], top[:, t, :], logits[:, t, :]).then_inc(s_topi, 1)

            def gate(i):
                g = 8 * i
                dve.wait_ge(s_topi, NT * i + NT)
                dve.tensor_copy(at[:], top_at[:, :, 0:2]).then_inc(s_gate, 1)
                dve.wait_ge(s_egap, i + 1)
                dve.tensor_scalar(wsum[:], expgap[:], 1.0, None, ALU.add).then_inc(s_gate, 1)
                dve.wait_ge(s_gate, g + 2)
                dve.reciprocal(wtop[:, 0, :], wsum[:]).then_inc(s_gate, 1)
                for k in range(2):
                    dve.tensor_tensor(pick[:, k, :, :], iota[:].unsqueeze(1).broadcast_to([P, NT, E]),
                                      at[:, :, k:k + 1].broadcast_to([P, NT, E]), ALU.is_equal).then_inc(s_gate, 1)
                dve.wait_ge(s_gate, g + 5)
                dve.tensor_tensor(wtop[:, 1, :], expgap[:], wtop[:, 0, :], ALU.mult).then_inc(s_gate, 1)
                dve.wait_ge(s_gate, g + 6)
                for k in range(2):
                    dve.tensor_tensor(pick[:, k, :, :], pick[:, k, :, :], along(wtop[:, k, :], [P, NT, E]),
                                      ALU.mult).then_inc(s_gate, 1)
                dve.wait_ge(s_gate, g + 8)
                dve.tensor_tensor(gates[:], pick[:, 0, :, :], pick[:, 1, :, :], ALU.add).then_inc(s_gates, 1)

            def hide(n, e, s):
                dve.wait_ge(s_up, 2 * E * n + 2 * e + s + 1)
                if s == 0:
                    dve.wait_ge(s_gall, E * n + e + 1)
                    dve.wait_ge(s_down, HIDDEN + E * n + e - HIDDEN + 1)
                dve.scalar_tensor_tensor(hidden[:, e % HIDDEN, s, :], up[s][:, 0:HALF], b1_neg[:, e:e + 1],
                                         gates_all[:, e, s * HALF:(s + 1) * HALF],
                                         ALU.max, ALU.mult).then_inc(s_hid, 1)

            def iteration(i, par, first, att, conv, ahead):
                for e in range(E):
                    if conv and e == 6:
                        keys_lo(i + 1)
                    if e not in POOLED:
                        hide(i - 1, e, 0)
                        hide(i - 1, e, 1)
                    elif not att:
                        dve.wait_ge(s_gall, E * (i - 1) + e + 1)
                        gate_hidden(dve, i - 1, e)
                    if att and e == 0:
                        reduce_max(i, 4)
                        reduce_max(i, 5)
                    if conv and e == 1:
                        centre(i + 1, 1 - par)
                    if att and e == 3:
                        add_probabilities(i, 1)
                    if att and e == 4:
                        add_probabilities(i, 2)
                        add_probabilities(i, 3)
                    if att and e == 5:
                        add_probabilities(i, 4)
                        add_probabilities(i, 5)
                    if conv and e == 4:
                        normalise(0, xn1[1 - par], cen0[1 - par], i + 1)
                    if conv and e == 7:
                        query_lo(i + 1)
                    if att and e == 7:
                        invert_denominators(i)
                    if att and e == 8:
                        scale_attention(i)
                        centre_sum(i, par)
                    if att and e == 10:
                        normalise(1, xn2[par], cen1, i)
                    if att and e == 11:
                        x2_lo(i, par)
                    if att and e == 12:
                        top_two(i)
                    if att and e == 13:
                        top_places(i)
                        gate(i)
                if conv:
                    for t in range(4):
                        reduce_max(i + 1, t)

            def opening():
                for t in range(NT):
                    reduce_max(0, t)
                mixture_weights()
                for t in range(1, 4):
                    add_probabilities(0, t)
                centre(1, 1)
                add_probabilities(0, 4)
                add_probabilities(0, 5)
                invert_denominators(0)
                scale_attention(0)
                centre_sum(0, 0)
                normalise(0, xn1[1], cen0[1], 1)
                keys_lo(1)
                normalise(1, xn2[0], cen1, 0)
                query_lo(1)
                x2_lo(0, 0)
                top_two(0)
                top_places(0)
                gate(0)
                bias_weights()
                for t in range(4):
                    reduce_max(1, t)

            pipeline(dve, opening, iteration)

            last = (BATCH - 1) % 2
            ft = small[:, 0:NT * D].rearrange("p (t c) -> p t c", c=D)
            dve.wait_ge(s_ft, CREDIT + BATCH)
            dve.wait_ge(s_res, CREDIT + BATCH - 1)
            dve.tensor_tensor(cen2[:, 0:FULL, :], ft[:, 0:FULL, :], xn2[last][:, 0:FULL, 0:D], ALU.add)
            dve.tensor_tensor(cen2[0:LAST, FULL:NT, :], ft[0:LAST, FULL:NT, :], xn2[last][0:LAST, FULL:NT, 0:D],
                              ALU.add).then_inc(s_cen[2], 1)
            dve.wait_ge(s_rstd[2], BATCH)
            dve.tensor_tensor(res[0][:], cen2[:], along(rstd[2][:], [P, NT, D]), ALU.mult).then_inc(s_tail, 1)
            dve.wait_ge(s_tail, 1)
            dve.tensor_tensor(res[1][:], res[0][:], gam[:].unsqueeze(1).broadcast_to([P, NT, D]),
                              ALU.mult).then_inc(s_tail, 1)
            dve.wait_ge(s_tail, 2)
            dve.wait_ge(s_fin, 3 * (BATCH - 1) + 1)
            dve.wait_ge(s_out, 16 * CREDIT + 64 * (BATCH - 1))
            dve.tensor_tensor(outs[:], res[1][:], res[2][:], ALU.add).then_inc(s_res, 1)

        @block.tensor
        def _(pe):
            def mm(dst, lhsT, rhs, start, stop):
                return pe.matmul(dst, lhsT, rhs, start=start, stop=stop, skip_group_check=True)

            pe.sem_inc(s_ft, CREDIT)
            pe.sem_inc(s_down, HIDDEN)
            pe.wait_ge(s_const, CONST)

            def transpose_x(n, part, dst):
                pe.wait_ge(s_x, 64 * (n + 1))
                lo = part * XT_TILES // 2
                for t in range(lo, lo + XT_TILES // 2):
                    w = P if t < XT_TILES - 1 else XT_LAST
                    last = pe.transpose(dst[:, (t - lo) * P:(t - lo) * P + w], xx[0:w, t, :], ident[0:w, 0:w])
                last.then_inc(s_xt, 1)

            def convolve(n, first, end, dst=small):
                if first == 0:
                    pe.wait_ge(s_xtc, 2 * n + 2)
                for k in range(first, end):
                    for s in range(2):
                        a = s * HALF + 2 * k
                        last = mm(dst[s * D:(s + 1) * D, 0:HALF], conv_w[:, k, :], xt[:, a:a + HALF],
                                  k == 0, k == CHUNKS - 1)
                if end == CHUNKS:
                    last.then_inc(s_conv, 1)

            def to_tokens(src, done, dst=small):
                for j in range(BLOCKS):
                    w = tile_size(2 * j)
                    last = pe.transpose(dst[0:w, j * P:(j + 1) * P], src[:, j * P:j * P + w], ident[:])
                last.then_inc(done, 1)

            def to_features(dst, src, done):
                for t in range(NT):
                    w, j = tile_size(t), t // 2
                    last = pe.transpose(dst[:, t % 2, j * P:j * P + w],
                                        src[0:w, t, 0:2 * D], ident[0:w, 0:w])
                last.then_inc(done, 1)

            def project(n):
                pe.wait_ge(s_khi, n + 1)
                pe.wait_ge(s_klo, n + 1)
                for s in range(2):
                    rhs = keys[:, s * HALF:(s + 1) * HALF]
                    mm(wide[0][:, s, 0:HALF], a_hi[:], rhs, True, False)
                    last = mm(wide[0][:, s, 0:HALF], a_lo[:], rhs, False, True)
                last.then_inc(s_q, 1)

            transpose_x(0, 0, up[0])
            transpose_x(0, 1, up[1])
            pe.wait_ge(s_wqk_in, 64)
            mm(wide[0][:, 0, 0:P], wq2[:].rearrange("o a d -> o (a d)"), wk2[:].rearrange("o a d -> o (a d)"),
               True, True).then_inc(s_a, 1)
            pe.wait_ge(s_weff, 3)
            for k in range(CHUNKS):
                last = pe.transpose(small[:, k * D:(k + 1) * D],
                                    w_eff[:, 2 * k:2 * k + 2, :].rearrange("o k i -> o (k i)"), ident[0:D, 0:D])
            last.then_inc(s_wt, 1)
            pe.wait_ge(s_wc, 1)
            convolve(0, 0, CHUNKS)
            pe.wait_ge(s_convc, 1)
            to_tokens(conv_t, s_ht)
            pe.wait_ge(s_ln[0], 1)
            to_features(wide[1], xn1[0], s_t1)
            pe.wait_ge(s_ahi, 1)
            pe.wait_ge(s_alo, 1)
            project(0)

            def max_scores(i, t, again=True):
                buf = 1 - t % 2
                if t == 0:
                    pe.wait_ge(s_qhi, i + 1)
                    pe.wait_ge(s_kone, i + 1)
                    pe.wait_ge(s_klo, i + 1)
                    if again:
                        pe.wait_ge(s_logit, 2 * i)
                elif t == 1:
                    pe.wait_ge(s_qlo, i + 1)
                    if again:
                        pe.wait_ge(s_gtc, i)
                elif t >= 2:
                    pe.wait_ge(s_max, NT * i + t - 1)
                a, w = tile_start(t), tile_size(t)
                lhs = q_hi[:, a:a + w]
                mm(wide[buf][0:w, 0, 0:HALF], lhs, keys[:, 0:HALF], True, True)
                mm(wide[buf][0:w, 1, 0:HALF], lhs, keys[:, TOK - HALF:TOK], True, True).then_inc(s_rough, 1)

            def bias_product():
                pe.wait_ge(s_b1, 3)
                pe.wait_ge(s_w2, 3)
                group = [e for e in range(E) if e not in POOLED]
                for e in group:
                    last = mm(mix[0:E, D:2 * D], b1_diag[:, e, :], w2s[:, e, :], e == group[0], e == group[-1])
                last.then_inc(s_bias, 1)

            def transpose_max(i):
                pe.wait_ge(s_max, NT * i + NT)
                for t in range(NT):
                    w, j = tile_size(t), t // 2
                    last = pe.transpose(wide[1][0:D + 1, t % 2, j * P:j * P + w], row_max[0:w, t, :], ident[0:w, 0:w])
                last.then_inc(s_maxt, 1)

            def scores(i, t):
                if t == 0:
                    pe.wait_ge(s_shift, i + 1)
                elif t >= 2:
                    pe.wait_ge(s_prob, NT * i + t - 1)
                a, w = tile_start(t), key_size(t)
                for s in range(2):
                    cols = slice(s * HALF, (s + 1) * HALF)
                    mm(wide[t % 2][0:w, s, 0:HALF], keys[:, a:a + w], q_hi[:, cols], True, False)
                    last = mm(wide[t % 2][0:w, s, 0:HALF], keys1[:, a:a + w], q_lo[:, cols], False, True)
                last.then_inc(s_score, 1)

            def weigh_values(i, t, buf):
                pe.wait_ge(s_prob, NT * i + t + 1)
                w = key_size(t)
                for s in range(2):
                    last = mm(small[s * D:(s + 1) * D, 0:HALF], xn1[buf][0:w, t, D:2 * D],
                              probs[0:w, t, s * HALF:(s + 1) * HALF], t == 0, t == NT - 1)
                if t == NT - 1:
                    last.then_inc(s_pv, 1)

            def denominators(i):
                pe.wait_ge(s_psum, (NT - 1) * (i + 1))
                for t in range(NT):
                    a, w = tile_start(t), tile_size(t)
                    last = mm(wide[1][0:w, 0, t:t + 1], prob_sum[:, a:a + w], ones[:], True, True)
                last.then_inc(s_den, 1)

            def attention_to_tokens(i):
                pe.wait_ge(s_pvc, i + 1)
                to_tokens(attn_t, s_at)

            def gate_logits(i, par):
                pe.wait_ge(s_x2lo, i + 1)
                pe.wait_ge(s_w1lo, 2)
                for t in range(NT):
                    a, w = tile_start(t), tile_size(t)
                    last = mm(wide[1][0:w, 0, 2 * t * E:2 * (t + 1) * E], x2[par][:, a:a + w],
                              gw[:].rearrange("p a e -> p (a e)"), True, True)
                last.then_inc(s_lg, 1)

            def transpose_gates(i):
                pe.wait_ge(s_gates, i + 1)
                for t in range(NT):
                    w, j = tile_size(t), t // 2
                    last = pe.transpose(wide[0][0:E, t % 2, j * P:j * P + w], gates[0:w, t, :], ident[0:w, 0:w])
                last.then_inc(s_gt, 1)

            def gated_biases(n):
                pe.wait_ge(s_biasw, 1)
                pe.wait_ge(s_gtc, n + 1)
                pe.wait_ge(s_mixc, CREDIT + n)
                for s in range(2):
                    last = mm(mix[s * D:(s + 1) * D, 0:HALF], bias_w[:], gates_t[:, s * HALF:(s + 1) * HALF],
                              True, False)
                last.then_inc(s_bmm, 1)

            def first_layer(n, e, buf):
                for s in range(2):
                    if e > 0 and e - 1 in POOLED:
                        pe.wait_ge(s_relu, hidden_before(n, e - 1, s, True))
                    elif e > 0:
                        pe.wait_ge(s_hid, hidden_before(n, e - 1, s, False))
                    rhs = x2[buf][:, s * HALF:(s + 1) * HALF]
                    mm(up[s][:, 0:HALF], w1_hi[:, e, :], rhs, True, False)
                    mm(up[s][:, 0:HALF], w1_lo[:, e, :], rhs, False, True).then_inc(s_up, 1)

            def second_layer(n, e):
                if e in POOLED:
                    pe.wait_ge(s_phid, CREDIT + hidden_before(n, e, 1, True))
                else:
                    pe.wait_ge(s_hid, hidden_before(n, e, 1, False))
                for s in range(2):
                    last = mm(mix[s * D:(s + 1) * D, 0:HALF], w2s[:, e, :], hidden[:, e % HIDDEN, s, :], False, e == E - 1)
                last.then_inc(s_down, 1)

            def iteration(i, par, first, att, conv, ahead):
                for e in range(E):
                    if e == 0:
                        gated_biases(i - 1)
                    first_layer(i - 1, e, 1 - par)
                    if ahead and 10 <= e < 13:
                        if e == 10:
                            pe.wait_ge(s_attn, 2 * i + 2)
                        convolve(i + 2, CONV_CUTS[e - 10], CONV_CUTS[e - 9])
                    if att and e == 11:
                        pe.wait_ge(s_ln[1], i + 1)
                        pe.wait_ge(s_rden, 2 * i + 2)
                        to_features(wide[1], xn2[par], s_t2)
                    if ahead and e == 12:
                        gate_logits(i, par)
                    if att and e == 15:
                        if ahead:
                            pe.wait_ge(s_xtc, 2 * i + 6)
                        elif conv:
                            pe.wait_ge(s_qhi, i + 2)
                            pe.wait_ge(s_qlo, i + 2)
                        transpose_gates(i)
                    for k in seconds_at(e):
                        second_layer(i - 1, k)
                    if att and e == 0:
                        max_scores(i, 4)
                        max_scores(i, 5)
                    if att and e == 1:
                        transpose_max(i)
                    if att and 2 <= e < 5:
                        scores(i, 2 * (e - 2))
                        scores(i, 2 * (e - 2) + 1)
                    if att and 5 <= e < 8:
                        if e == 5:
                            pe.wait_ge(s_ftc, CREDIT + i - 1)
                        weigh_values(i, 2 * (e - 5), par)
                        weigh_values(i, 2 * (e - 5) + 1, par)
                    if conv and e == 5:
                        pe.wait_ge(s_ln[0], i + 2)
                        pe.wait_ge(s_prob, NT * i + NT)
                        to_features(wide[1], xn1[1 - par], s_t1)
                    if conv and e == 6:
                        project(i + 1)
                    if att and e == 7:
                        if conv:
                            pe.wait_ge(s_kone, i + 2)
                            pe.wait_ge(s_klo, i + 2)
                        denominators(i)
                    if att and e == 8:
                        attention_to_tokens(i)
                    if ahead and e == 8:
                        pe.wait_ge(s_qhi, i + 2)
                        pe.wait_ge(s_qlo, i + 2)
                        transpose_x(i + 2, 0, wide[0][:, 0, :])
                        transpose_x(i + 2, 1, wide[0][:, 1, :])
                    if att and not ahead and e == 12:
                        gate_logits(i, par)
                    if ahead and e == 14:
                        pe.wait_ge(s_convc, i + 3)
                        to_tokens(conv_t, s_ht)
                    if conv and e == 14:
                        max_scores(i + 1, 0)
                if conv:
                    max_scores(i + 1, 1)
                for k in seconds_at(E):
                    second_layer(i - 1, k)
                if conv:
                    max_scores(i + 1, 2)
                    max_scores(i + 1, 3)
                pe.wait_ge(s_mixc, CREDIT + i)
                if ahead:
                    pe.wait_ge(s_h0, i + 3)
                elif att:
                    pe.wait_ge(s_attn, 2 * i + 2)
                to_tokens(moe_t, s_ft)

            def opening():
                for t in range(NT):
                    max_scores(0, t, False)
                transpose_x(1, 0, up[0])
                transpose_x(1, 1, up[1])
                pe.wait_ge(s_moe_in, 16 * MOE_LOADS)
                pe.transpose(mix[:, 0:E], b1_rows[:], ident[0:E, 0:E]).then_inc(s_b1t, 1)
                transpose_max(0)
                for k in range(3):
                    convolve(1, CONV_CUTS[k], CONV_CUTS[k + 1], up[0])
                    scores(0, 2 * k)
                    scores(0, 2 * k + 1)
                pe.wait_ge(s_convc, 2)
                to_tokens(conv_t, s_ht, up[1])
                for t in range(NT):
                    weigh_values(0, t, 0)
                denominators(0)
                attention_to_tokens(0)
                pe.wait_ge(s_h0, 2)
                transpose_x(2, 0, up[0])
                transpose_x(2, 1, up[1])
                pe.wait_ge(s_ln[0], 2)
                pe.wait_ge(s_rden, 2)
                to_features(wide[1], xn1[1], s_t1)
                project(1)
                pe.wait_ge(s_ln[1], 1)
                pe.wait_ge(s_kone, 2)
                to_features(wide[1], xn2[0], s_t2)
                convolve(2, 0, 1, up[0])
                gate_logits(0, 0)
                convolve(2, 1, 4, up[0])
                bias_product()
                pe.wait_ge(s_qhi, 2)
                pe.wait_ge(s_qlo, 2)
                transpose_gates(0)
                max_scores(1, 0)
                max_scores(1, 1)
                convolve(2, 4, CHUNKS, up[0])
                max_scores(1, 2)
                max_scores(1, 3)
                pe.wait_ge(s_convc, 3)
                to_tokens(conv_t, s_ht, up[1])
                pe.wait_ge(s_h0, 3)

            pipeline(pe, opening, iteration)


INPUTS = ["x", "L0_tok_w_real", "L0_tok_w_imag", "L0_tok_phases", "L0_attn_Wq", "L0_attn_Wk", "L0_ffn_gate_w",
          "L0_ffn_gate_b", "L0_ffn_w1", "L0_ffn_b1", "L0_ffn_w2", "L0_ffn_b2", "L0_ffn_gamma", "L0_ffn_beta"]


def kernel(**inputs):
    import numpy as np
    import concourse.bacc as bacc
    from concourse.bass_utils import run_bass_kernel_spmd

    nc = bacc.Bacc("TRN2", target_bir_lowering=False, num_devices=1)
    arrays, args = {}, []
    for name in INPUTS:
        a = np.ascontiguousarray(inputs[name])
        arrays[name] = a
        args.append(nc.dram_tensor(name, a.shape, F32, kind="ExternalInput").ap())
    out = nc.dram_tensor("out", (BATCH, TOK, D), F32, kind="ExternalOutput").ap()
    build(nc, *args, out)
    r = run_bass_kernel_spmd(nc, [arrays], core_ids=[0])
    return r.results[0]["out"]
```
